# Optimizing a Trainium2 kernel written in Bass

```python
import numpy as np
import jax
import jax.numpy as jnp

def _softmax(x, axis=-1):
    return jax.nn.softmax(x, axis=axis)

def _gelu(x):
    return jax.nn.gelu(x, approximate=True)

def _silu(x):
    return jax.nn.silu(x)

def _sigmoid(x):
    return jax.nn.sigmoid(x)

def _layernorm(x, axis=-1, eps=1e-05):
    m = jnp.mean(x, axis=axis, keepdims=True)
    v = jnp.var(x, axis=axis, keepdims=True)
    return (x - m) / jnp.sqrt(v + eps)

def _scatter_add(tgt, idx, src, axis=0):
    return tgt.at[idx].add(src)

def _segment_sum(src, seg, n):
    return jax.ops.segment_sum(src, seg, n)
kernel_name = 'mk_vit_tower_d1_tok_img512_r4_8ef23f'

def setup_inputs(seed: int=0):
    np.random.seed(seed)
    _w = jnp.asarray

    def _rec_inputs():
        import jax
        import jax.numpy as jnp
        _rk = jax.random.key(seed)
        x = 7.57192e-06 + 1.00007 * jax.random.normal(jax.random.fold_in(_rk, 1), (64, 3, 224, 224), jnp.float32)
        return x
    x = _rec_inputs()

    def _L0_tok_setup():
        import jax, jax.numpy as jnp
        import numpy as np
        DEPTH = 4
        HEADS = 8
        DIM = 128
        HID = 256
        P = 16
        IMG = 224
        GRID = IMG // P
        NPATCH = GRID * GRID
        NTOK = NPATCH + 1
        BATCH = 64
        EPS = 1e-05

        def layernorm(x, w, b):
            mu = jnp.mean(x, axis=-1, keepdims=True)
            var = jnp.mean(jnp.square(x - mu), axis=-1, keepdims=True)
            return (x - mu) * jax.lax.rsqrt(var + EPS) * w + b
        key = jax.random.key(seed)
        ks = jax.random.split(key, 12)
        s = 0.02
        inp = {'x': jax.random.normal(ks[0], (BATCH, 3, IMG, IMG), jnp.float32), 'conv_w': jax.random.normal(ks[1], (3 * P * P, DIM), jnp.float32) * s, 'conv_b': jnp.zeros((DIM,), jnp.float32), 'cls_token': jax.random.normal(ks[2], (1, 1, DIM), jnp.float32) * s, 'pos_embed': jax.random.normal(ks[3], (1, NTOK, DIM), jnp.float32) * s, 'ln1_w': jnp.ones((DEPTH, DIM), jnp.float32), 'ln1_b': jnp.zeros((DEPTH, DIM), jnp.float32), 'qkv_w': jax.random.normal(ks[4], (DEPTH, DIM, 3 * DIM), jnp.float32) * s, 'qkv_b': jnp.zeros((DEPTH, 3 * DIM), jnp.float32), 'proj_w': jax.random.normal(ks[5], (DEPTH, DIM, DIM), jnp.float32) * s, 'proj_b': jnp.zeros((DEPTH, DIM), jnp.float32), 'ln2_w': jnp.ones((DEPTH, DIM), jnp.float32), 'ln2_b': jnp.zeros((DEPTH, DIM), jnp.float32), 'fc1_w': jax.random.normal(ks[6], (DEPTH, DIM, HID), jnp.float32) * s, 'fc1_b': jnp.zeros((DEPTH, HID), jnp.float32), 'fc2_w': jax.random.normal(ks[7], (DEPTH, HID, DIM), jnp.float32) * s, 'fc2_b': jnp.zeros((DEPTH, DIM), jnp.float32), 'norm_w': jnp.ones((DIM,), jnp.float32), 'norm_b': jnp.zeros((DIM,), jnp.float32)}
        return inp
    _L0_tok_all = _L0_tok_setup()
    _L0_tok_in = {k: v for k, v in _L0_tok_all.items() if k in ('conv_w', 'conv_b', 'cls_token', 'pos_embed', 'ln1_w', 'ln1_b', 'qkv_w', 'qkv_b', 'proj_w', 'proj_b', 'ln2_w', 'ln2_b', 'fc1_w', 'fc1_b', 'fc2_w', 'fc2_b', 'norm_w', 'norm_b')}
    del _L0_tok_all

    def _L0_attn_setup():
        import jax, jax.numpy as jnp
        import numpy as np
        GAMMA = 1.0
        key = jax.random.key(seed)
        x = jax.random.normal(key, (4, 512, 128), dtype=jnp.float32)
        return {'x': x}
    _L0_attn_all = _L0_attn_setup()
    _L0_attn_in = {k: v for k, v in _L0_attn_all.items() if k in ()}
    del _L0_attn_all

    def _L0_ffn_setup():
        import jax, jax.numpy as jnp
        import numpy as np
        B, T, D = (4, 2048, 128)
        E, F, CAP = (8, 512, 1024)
        key = jax.random.key(seed)
        ks = jax.random.split(key, 6)
        s = 0.02
        return {'x': jax.random.normal(ks[0], (B, T, D), dtype=jnp.float32), 'Wr': jax.random.normal(ks[1], (D, E), dtype=jnp.float32) * s, 'W1': jax.random.normal(ks[2], (E, D, F), dtype=jnp.float32) * s, 'b1': jax.random.normal(ks[3], (E, F), dtype=jnp.float32) * s, 'W2': jax.random.normal(ks[4], (E, F, D), dtype=jnp.float32) * s, 'b2': jax.random.normal(ks[5], (E, D), dtype=jnp.float32) * s}
    _L0_ffn_all = _L0_ffn_setup()
    _L0_ffn_in = {k: v for k, v in _L0_ffn_all.items() if k in ('Wr', 'W1', 'b1', 'W2', 'b2')}
    del _L0_ffn_all
    return {'x': x, 'L0_tok_conv_w': _L0_tok_in['conv_w'], 'L0_tok_conv_b': _L0_tok_in['conv_b'], 'L0_tok_cls_token': _L0_tok_in['cls_token'], 'L0_tok_pos_embed': _L0_tok_in['pos_embed'], 'L0_tok_ln1_w': _L0_tok_in['ln1_w'], 'L0_tok_ln1_b': _L0_tok_in['ln1_b'], 'L0_tok_qkv_w': _L0_tok_in['qkv_w'], 'L0_tok_qkv_b': _L0_tok_in['qkv_b'], 'L0_tok_proj_w': _L0_tok_in['proj_w'], 'L0_tok_proj_b': _L0_tok_in['proj_b'], 'L0_tok_ln2_w': _L0_tok_in['ln2_w'], 'L0_tok_ln2_b': _L0_tok_in['ln2_b'], 'L0_tok_fc1_w': _L0_tok_in['fc1_w'], 'L0_tok_fc1_b': _L0_tok_in['fc1_b'], 'L0_tok_fc2_w': _L0_tok_in['fc2_w'], 'L0_tok_fc2_b': _L0_tok_in['fc2_b'], 'L0_tok_norm_w': _L0_tok_in['norm_w'], 'L0_tok_norm_b': _L0_tok_in['norm_b'], 'L0_ffn_Wr': _L0_ffn_in['Wr'], 'L0_ffn_W1': _L0_ffn_in['W1'], 'L0_ffn_b1': _L0_ffn_in['b1'], 'L0_ffn_W2': _L0_ffn_in['W2'], 'L0_ffn_b2': _L0_ffn_in['b2']}

def reference(x, L0_tok_conv_w, L0_tok_conv_b, L0_tok_cls_token, L0_tok_pos_embed, L0_tok_ln1_w, L0_tok_ln1_b, L0_tok_qkv_w, L0_tok_qkv_b, L0_tok_proj_w, L0_tok_proj_b, L0_tok_ln2_w, L0_tok_ln2_b, L0_tok_fc1_w, L0_tok_fc1_b, L0_tok_fc2_w, L0_tok_fc2_b, L0_tok_norm_w, L0_tok_norm_b, L0_ffn_Wr, L0_ffn_W1, L0_ffn_b1, L0_ffn_W2, L0_ffn_b2):
    import jax
    import jax.numpy as jnp

    def _L0_tok_ref(x, conv_w, conv_b, cls_token, pos_embed, ln1_w, ln1_b, qkv_w, qkv_b, proj_w, proj_b, ln2_w, ln2_b, fc1_w, fc1_b, fc2_w, fc2_b, norm_w, norm_b):
        import jax, jax.numpy as jnp
        import numpy as np
        DEPTH = 4
        HEADS = 8
        DIM = 128
        HID = 256
        P = 16
        IMG = 224
        GRID = IMG // P
        NPATCH = GRID * GRID
        NTOK = NPATCH + 1
        BATCH = 64
        EPS = 1e-05

        def layernorm(x, w, b):
            mu = jnp.mean(x, axis=-1, keepdims=True)
            var = jnp.mean(jnp.square(x - mu), axis=-1, keepdims=True)
            return (x - mu) * jax.lax.rsqrt(var + EPS) * w + b
        B = x.shape[0]
        hd = DIM // HEADS
        scale = hd ** (-0.5)
        patches = x.reshape(B, 3, GRID, P, GRID, P)
        patches = patches.transpose(0, 2, 4, 1, 3, 5).reshape(B, NPATCH, 3 * P * P)
        tok = patches @ conv_w + conv_b
        cls = jnp.broadcast_to(cls_token, (B, 1, DIM))
        h = jnp.concatenate([cls, tok], axis=1) + pos_embed
        for i in range(DEPTH):
            y = layernorm(h, ln1_w[i], ln1_b[i])
            qkv = (y @ qkv_w[i] + qkv_b[i]).reshape(B, NTOK, 3, HEADS, hd)
            qkv = qkv.transpose(2, 0, 3, 1, 4)
            q, k, v = (qkv[0], qkv[1], qkv[2])
            attn = jax.nn.softmax(jnp.einsum('bhnd,bhmd->bhnm', q, k) * scale, axis=-1)
            o = jnp.einsum('bhnm,bhmd->bhnd', attn, v)
            o = o.transpose(0, 2, 1, 3).reshape(B, NTOK, DIM)
            h = h + (o @ proj_w[i] + proj_b[i])
            y = layernorm(h, ln2_w[i], ln2_b[i])
            y = jax.nn.gelu(y @ fc1_w[i] + fc1_b[i], approximate=False)
            h = h + (y @ fc2_w[i] + fc2_b[i])
        return layernorm(h, norm_w, norm_b)

    def _L0_attn_ref(x):
        import jax, jax.numpy as jnp
        import numpy as np
        GAMMA = 1.0
        sq = jnp.sum(x * x, axis=-1)
        dots = jnp.einsum('bse,bte->bst', x, x)
        dist2 = sq[:, :, None] + sq[:, None, :] - 2.0 * dots
        dist2 = jnp.maximum(dist2, 0.0)
        K = jnp.exp(-GAMMA * dist2)
        attn = jax.nn.softmax(K, axis=-1)
        return jnp.einsum('bst,bte->bse', attn, x)

    def _L0_ffn_ref(x, Wr, W1, b1, W2, b2):
        import jax, jax.numpy as jnp
        import numpy as np
        B, T, D = (4, 2048, 128)
        E, F, CAP = (8, 512, 1024)
        Bb, Tt, Dd = x.shape
        N = Bb * Tt
        C = min(CAP, N)
        x_flat = x.reshape(N, Dd)
        logits = x_flat @ Wr
        probs = jax.nn.softmax(logits, axis=0)
        vals, idx = jax.lax.top_k(probs.T, C)
        selected = x_flat[idx]
        h = jax.nn.gelu(jnp.einsum('ecd,edf->ecf', selected, W1) + b1[:, None, :], approximate=False)
        out_e = jnp.einsum('ecf,efd->ecd', h, W2) + b2[:, None, :]
        weighted = vals[..., None] * out_e
        output = jnp.zeros_like(x_flat).at[idx.reshape(-1)].add(weighted.reshape(-1, Dd))
        return output.reshape(Bb, Tt, Dd)
    h = _L0_tok_ref(x, L0_tok_conv_w, L0_tok_conv_b, L0_tok_cls_token, L0_tok_pos_embed, L0_tok_ln1_w, L0_tok_ln1_b, L0_tok_qkv_w, L0_tok_qkv_b, L0_tok_proj_w, L0_tok_proj_b, L0_tok_ln2_w, L0_tok_ln2_b, L0_tok_fc1_w, L0_tok_fc1_b, L0_tok_fc2_w, L0_tok_fc2_b, L0_tok_norm_w, L0_tok_norm_b)
    h = h + _L0_attn_ref(_layernorm(h, axis=-1))
    h = h + _L0_ffn_ref(_layernorm(h, axis=-1), L0_ffn_Wr, L0_ffn_W1, L0_ffn_b1, L0_ffn_W2, L0_ffn_b2)
    return h

_drawn_inputs = setup_inputs


def setup_inputs(seed=0):
    import zlib

    import numpy as np

    out = dict(_drawn_inputs(seed))
    spreads = {'L0_tok_conv_b': (0.0, 0.1),
     'L0_tok_ln1_w': (1.0, 0.6),
     'L0_tok_ln1_b': (0.0, 0.327),
     'L0_tok_qkv_b': (0.0, 0.1),
     'L0_tok_proj_b': (0.0, 0.1),
     'L0_tok_ln2_w': (1.0, 0.6),
     'L0_tok_ln2_b': (0.0, 0.469),
     'L0_tok_fc1_b': (0.0, 0.1),
     'L0_tok_fc2_b': (0.0, 0.1),
     'L0_tok_norm_w': (1.0, 0.2),
     'L0_tok_norm_b': (0.0, 0.1)}
    factors = {'L0_tok_cls_token': 8.0,
     'L0_ffn_Wr': 64.0,
     'L0_ffn_W1': 64.0,
     'L0_ffn_b1': 64.0,
     'L0_ffn_W2': 64.0,
     'L0_ffn_b2': 64.0}
    for name, (base, spread) in spreads.items():
        noise = np.random.default_rng([zlib.crc32(name.encode()), seed]).standard_normal(out[name].shape)
        drawn = base * np.exp(spread * noise) if base else spread * noise
        out[name] = jnp.asarray(drawn.astype(out[name].dtype))
    for name, factor in factors.items():
        out[name] = (out[name] * factor).astype(out[name].dtype)
    return out
```

```python
def build(nc, A, out):
    import concourse.bass as bass
    from concourse import mybir
    from contextlib import ExitStack

    f32, bf16, i32 = mybir.dt.float32, mybir.dt.bfloat16, mybir.dt.int32
    ALU = mybir.AluOpType
    ACT = mybir.ActivationFunctionType
    AX = mybir.AxisListType

    IMAGES, NTOK, D = out.shape
    DEPTH = A["ln1_w"].shape[0]
    HID = A["fc1_w"].shape[2]
    HEADS = 8
    HD = D // HEADS
    R = (NTOK + 1) // 2
    P1 = R - 1
    W = 2 * R
    W2 = 2 * W
    PAIRS = IMAGES // 2
    TILES = 2 * IMAGES
    CH = A["x"].shape[0]
    EPS = 1e-5
    SCALE = float(HD) ** -0.5
    NP = 8
    NB = 4
    NZ = 4

    top = ExitStack()
    with top:
        def scope_tools(stack):
            def sb(name, shape, dt=f32):
                return stack.enter_context(nc.sbuf_tensor(name, shape, dt))

            def pb(name, shape, dt=f32):
                return stack.enter_context(nc.psum_tensor(name, shape, dt))

            def sem(name):
                return stack.enter_context(nc.semaphore(name))
            return sb, pb, sem

        sb, pb, sem = scope_tools(top)
        h = sb("h", [R, TILES, D])
        ident = sb("ident", [128, 128])
        ones = sb("ones", [128, 128])
        passed = sem("passed")
        with ExitStack() as st:
            sb, pb, sem = scope_tools(st)
            NX = 3
            xt = sb("xt", [128, NX, CH, 4 * P1])
            wconv = sb("wconv", [128, CH, D])
            pos = sb("pos", [P1, 2, D])
            convb = sb("convb", [P1, D])
            posb = sb("posb", [P1, 2, D])
            cls = sb("cls", [1, 2, D])
            clsrow = sb("clsrow", [1, D])
            acc = pb("acc", [128, 2, 4, D])

            x_in = [sem(f"x_in{i}") for i in range(NX)]
            w_in, consts_in, tok_ready, tok_taken = sem("w_in"), sem("consts_in"), sem("tok_ready"), sem("tok_taken")
            posb_ready, cls_ready, cls_out, ident_zero = sem("posb_ready"), sem("cls_ready"), sem("cls_out"), sem("ident_zero")

            block = st.enter_context(nc.Block())

            @block.sync
            def _(sp):
                sp.dma_start(wconv[:, :, :], A["conv_w"].rearrange("(c p) d -> p c d", p=128)).then_inc(w_in, 16)

                def load(pair, slot):
                    sp.dma_start(xt[:, slot, :, :], A["x"][:, :, bass.ds(pair * (4 * P1), 4 * P1)]
                                 .rearrange("c p n -> p c n")).then_inc(x_in[slot], 16)

                for i in range(NX):
                    load(i, i)
                with sp.Fori(0, PAIRS // NX - 1) as q:
                    for u in range(NX):
                        sp.wait_ge(tok_ready, q * NX + (u + 1))
                        load(q * NX + (NX + u), u)
                for i in range(PAIRS // NX * NX, PAIRS):
                    sp.wait_ge(tok_ready, i - NX + 1)
                    load(i, i % NX)
                sp.wait_ge(cls_ready, 1)
                sp.dma_start(h[P1:R, :, :], clsrow[0:1, :].rearrange("p (a d) -> p a d", a=1)
                             .to_broadcast([1, TILES, D])).then_inc(cls_out, 16)
                sp.wait_ge(cls_out, 16)

            @block.scalar
            def _(act):
                act.dma_start(pos[:, :, :], A["pos_embed"][0, 1:NTOK, :].rearrange("(t p) d -> p t d", p=P1)).then_inc(consts_in, 16)
                act.dma_start(convb[:, :], A["conv_b"].partition_broadcast(P1)).then_inc(consts_in, 16)
                act.dma_start(cls[:, 0, :], A["cls_token"][0]).then_inc(consts_in, 16)
                act.dma_start(cls[:, 1, :], A["pos_embed"][0, 0:1, :]).then_inc(consts_in, 16)

            @block.gpsimd
            def _(pool):
                pool.memset(ones[:, :], 1.0)
                pool.memset(ident[:, :], 0.0).then_inc(ident_zero, 1)
                pool.wait_ge(ident_zero, 1)
                pool.affine_select(out=ident[:, :], in_=ident[:, :], compare_op=ALU.not_equal, fill=1.0,
                                   base=0, pattern=[[-1, 128]], channel_multiplier=1)

            @block.tensor
            def _(pe):
                pe.wait_ge(w_in, 16)

                def embed(slot, b):
                    for t in range(4):
                        for c in range(CH):
                            last = pe.matmul(acc[0:P1, b, t, :], xt[:, slot, c, t * P1:(t + 1) * P1], wconv[:, c, :],
                                             start=(c == 0), stop=(c == CH - 1))
                    last.then_inc(tok_ready, 1)

                for i in range(2):
                    pe.wait_ge(x_in[i], 16)
                    embed(i, i)
                with pe.Fori(0, (PAIRS - 2) // 6) as q:
                    for u in range(6):
                        slot = (u + 2) % NX
                        pe.wait_ge(x_in[slot], q * 32 + 16 * ((u + 2) // NX + 1))
                        pe.wait_ge(tok_taken, q * 6 + (u + 1))
                        embed(slot, u % 2)

            @block.vector
            def _(dve):
                dve.wait_ge(consts_in, 64)
                for t in range(2):
                    last = dve.tensor_tensor(posb[:, t, :], pos[:, t, :], convb[:, :], ALU.add)
                last.then_inc(posb_ready, 1)
                dve.tensor_tensor(clsrow[:, :], cls[:, 0, :], cls[:, 1, :], ALU.add).then_inc(cls_ready, 1)
                dve.wait_ge(posb_ready, 1)
                with dve.Fori(0, PAIRS // 2) as q:
                    for b in range(2):
                        dve.wait_ge(tok_ready, q * 2 + (b + 1))
                        dve.wait_ge(posb_ready, 1)
                        for im in range(2):
                            last = dve.tensor_tensor(h[0:P1, bass.ds(q * 8 + (4 * b + 2 * im), 2), :],
                                                     acc[0:P1, b, 2 * im:2 * im + 2, :], posb[:, :, :], ALU.add)
                        last.then_inc(tok_taken, 1)
        with ExitStack() as st:
            sb, pb, sem = scope_tools(st)
            wqkv_raw = sb("wqkv_raw", [128, 3 * D])
            wproj_raw = sb("wproj_raw", [128, D])
            wfc1_raw = sb("wfc1_raw", [128, HID])
            wfc2_raw = sb("wfc2_raw", [128, 2, D])
            cols = sb("cols", [128, 4])
            qkvb = sb("qkvb", [128, 3])
            fc1b = sb("fc1b", [128, 2])
            rows = sb("rows", [1, 2, D])
            wqkv = sb("wqkv", [128, 3 * D])
            wproj = sb("wproj", [128, D])
            wfc1 = sb("wfc1", [128, HID])
            wfc2 = sb("wfc2", [128, 2, D])
            bqkv = sb("bqkv", [128, 3])
            bfc1 = sb("bfc1", [128, 2])
            bv_wide = sb("bv_wide", [128, R])
            bproj = sb("bproj", [R, D])
            bfc2 = sb("bfc2", [R, D])

            eps_t = sb("eps_t", [R, 4])
            mhalf = sb("mhalf", [R, 4])
            stats = sb("stats", [R, 4, 6])
            mv = sb("mv", [R, 4, 2])
            rstd = sb("rstd", [R, 4])
            xc = sb("xc", [R, 4, D])
            y = sb("y", [R, 4, D])
            yT = sb("yT", [128, W2])
            parts = sb("parts", [128, 2, 3, W2], bf16)
            rest = sb("rest", [128, 2, W2])
            Q = sb("Q", [98, NB, HEADS, W2], bf16)
            K = sb("K", [98, NB, HEADS, W2], bf16)
            V = sb("V", [R, NB, 4, HEADS, 32])
            negmax = sb("negmax", [R, 2, 2, HEADS])
            mhi = sb("mhi", [2 * HEADS, 2, R], bf16)
            mlo = sb("mlo", [2 * HEADS, 2, R], bf16)
            probs = sb("probs", [R, NP, 2 * W])
            rsum = sb("rsum", [R, 2 * HEADS])
            oU = sb("oU", [128, 2 * W])
            o = sb("o", [R, 2, D])
            oT = sb("oT", [128, W])
            z = sb("z", [R, NZ, 4, D])
            zT = sb("zT", [128, 2, W2])
            hid = sb("hid", [128, 2, 2, W2])
            q_scratch = nc.dram_tensor("q_scratch", [HEADS, 3, HD, W2], bf16, kind="Internal").ap()
            k_scratch = nc.dram_tensor("k_scratch", [3, HEADS, HD, W2], bf16, kind="Internal").ap()

            ps = pb("ps", [128, 8, 512])

            raw_in, folded, prep_mm = sem("raw_in"), sem("folded"), sem("prep_mm")
            bias_ready, bvw_ready, consts = sem("bias_ready"), sem("bvw_ready"), sem("consts")
            weights_ready = sem("weights_ready")
            ln_stats, ln_aggr, ln_var, ln_rstd, ln_centred, y_ready = (sem(n) for n in (
                "ln_stats", "ln_aggr", "ln_var", "ln_rstd", "ln_centred", "y_ready"))
            hbias = sem("hbias")
            yT_ps, yT_ready = sem("yT_ps"), sem("yT_ready")
            qk_ps, part1, rest_ready, part2, parts_ready = (sem(n) for n in (
                "qk_ps", "part1", "rest_ready", "part2", "parts_ready"))
            qk_saved, qk_loaded = [sem("q_saved"), sem("k_saved")], sem("qk_loaded")
            v_ps, v_ready = sem("v_ps"), sem("v_ready")
            mx_ps, mx_done = sem("mx_ps"), sem("mx_done")
            mT_ps, mhi_ready, mlo_ready = sem("mT_ps"), sem("mhi_ready"), sem("mlo_ready")
            max_loaded = [sem("max_loaded0"), sem("max_loaded1")]
            st_ps, probs_ready, probs_used = sem("st_ps"), sem("probs_ready"), sem("probs_used")
            oU_ready, oU_turned, rsum_ready, o_ready = sem("oU_ready"), sem("oU_turned"), sem("rsum_ready"), sem("o_ready")
            oT_ps, oT_ready, proj_ps, attn_done = (sem(n) for n in ("oT_ps", "oT_ready", "proj_ps", "attn_done"))
            ln2_stats, ln2_aggr, ln2_var, ln2_rstd, ln2_centred, z_ready, hbias2 = (sem(n) for n in (
                "ln2_stats", "ln2_aggr", "ln2_var", "ln2_rstd", "ln2_centred", "z_ready", "hbias2"))
            zT_ps, zT_ready, hid_ps, hid_ready, fc2_ps, mlp_done = (sem(n) for n in (
                "zT_ps", "zT_ready", "hid_ps", "hid_ready", "fc2_ps", "mlp_done"))

            block = st.enter_context(nc.Block())

            def slots(engine, layer, body):
                def on(k):
                    return {n for n, lag in (("norm", 4), ("project", 3), ("maxima", 1), ("now", 0), ("tail", -1))
                            if 0 <= k + lag < PAIRS}
                for k in range(-4, 1):
                    body(k, k % NB, on(k))
                with engine.Fori(0, (PAIRS - 5) // NB) as q:
                    for u in range(NB):
                        body(q * NB + (u + 1), (u + 1) % NB, on(1))
                for k in range(1 + (PAIRS - 5) // NB * NB, PAIRS + 1):
                    body(k, k % NB, on(k))


            def bank_T(b, s):
                bank = (2 * HEADS * b + s) % 3
                before = [(2 * HEADS * ((b - 1) % NB if e < 0 else b) + e % (2 * HEADS)) % 3 for e in range(s - 1, s - 5, -1)]
                return bank, before.index(bank) + 1

            MISC = [("mT1", "now"), ("proj0", "tail"), ("yT", "project"), ("q", "project"), ("k", "project"), ("oT1", "tail"),
                    ("mT0", "maxima"), ("proj1", "tail"), ("v", "project"), ("oT0", "now")]
            LEAD = {"project": 3, "maxima": 1, "now": 0, "tail": -1}

            @block.sync
            def _(sp):
                with sp.Fori(0, DEPTH) as l:
                    sp.wait_ge(weights_ready, l)
                    sp.dma_start(wqkv_raw[:, :], A["qkv_w"][l]).then_inc(raw_in, 16)
                    sp.dma_start(wproj_raw[:, :], A["proj_w"][l]).then_inc(raw_in, 16)
                    sp.dma_start(wfc1_raw[:, :], A["fc1_w"][l]).then_inc(raw_in, 16)
                    sp.dma_start(wfc2_raw[:, :, :], A["fc2_w"][l].rearrange("(c p) d -> p c d", p=128)).then_inc(raw_in, 16)
                    for i, n in enumerate(("ln1_w", "ln1_b", "ln2_w", "ln2_b")):
                        sp.dma_start(cols[:, i:i + 1], A[n][l].rearrange("(p a) -> p a", a=1)).then_inc(raw_in, 16)
                    for i in range(3):
                        sp.dma_start(qkvb[:, i:i + 1], A["qkv_b"][l, i * D:(i + 1) * D].rearrange("(p a) -> p a", a=1)).then_inc(raw_in, 16)
                    for i in range(2):
                        sp.dma_start(fc1b[:, i:i + 1], A["fc1_b"][l, i * D:(i + 1) * D].rearrange("(p a) -> p a", a=1)).then_inc(raw_in, 16)
                    sp.dma_start(rows[:, 0, :], A["proj_b"][l].rearrange("(a p) -> a p", a=1)).then_inc(raw_in, 16)
                    sp.dma_start(rows[:, 1, :], A["fc2_b"][l].rearrange("(a p) -> a p", a=1)).then_inc(raw_in, 16)

                    def load_max(b, im, n):
                        sp.wait_ge(mlo_ready, n)
                        for i, m in enumerate((mhi, mlo)):
                            for t in range(2):
                                sp.dma_start(Q[96 + i:97 + i, b, :, im * W + t * R:im * W + (t + 1) * R],
                                             m[t * HEADS:(t + 1) * HEADS, im, :]).then_inc(max_loaded[im], 16)

                    def body(k, b, on):
                        it = l * PAIRS + k
                        b1, b3 = (b + 1) % NB, (b + 3) % NB
                        if "now" in on:
                            load_max(b, 1, it * 2 + 2)
                        if "project" in on:
                            n = it + 3
                            sp.wait_ge(qk_loaded, n * 144)
                            sp.wait_ge(parts_ready, n * 2 + 1)
                            for j in range(3):
                                sp.dma_start(q_scratch[:, j, :, :], parts[:, 0, j, :]).then_inc(qk_saved[0], 16)
                        if "maxima" in on:
                            load_max(b1, 0, it * 2 + 3)
                        if "project" in on:
                            sp.wait_ge(parts_ready, n * 2 + 2)
                            sp.dma_start(k_scratch.rearrange("j h d t -> (h d) j t"), parts[:, 1, :, :]).then_inc(qk_saved[1], 16)
                            if "tail" in on:
                                sp.wait_ge(st_ps, it * 2 * HEADS)
                            sp.wait_ge(qk_saved[0], n * 48 + 48)
                            for r0, j0, m in ((0, 0, 3), (48, 0, 2), (80, 0, 1)):
                                sp.dma_start(Q[r0:r0 + m * HD, b3, :, :], q_scratch[:, j0:j0 + m].rearrange("h j d t -> (j d) h t")).then_inc(qk_loaded, 16)
                            sp.wait_ge(qk_saved[1], n * 16 + 16)
                            for r, j in enumerate((0, 0, 0, 1, 1, 2)):
                                sp.dma_start(K[r * HD:(r + 1) * HD, b3, :, :], k_scratch[j].rearrange("h d t -> d h t")).then_inc(qk_loaded, 16)
                    slots(sp, l, body)

            @block.gpsimd
            def _(pool):
                pool.memset(eps_t[:, :], EPS)
                pool.memset(mhalf[:, :], -0.5)
                pool.memset(V[:, :, :, :, :], 1.0).then_inc(consts, 1)
                pool.wait_ge(consts, 1)
                pool.memset(K[96:98, :, :, :], 1.0).then_inc(consts, 1)
                pool.wait_ge(consts, 2)

                def normalise(pair, n, s_aggr, s_var, s_rstd, s_centred, s_out, s_bias, dst, dst_free, bias_row):
                    pool.wait_ge(s_out, n - 1)
                    pool.wait_ge(s_aggr, n)
                    pool.tensor_tensor(rstd[:, :], mv[:, :, 1], eps_t[:, :], ALU.add).then_inc(s_var, 1)
                    pool.wait_ge(s_var, n)
                    pool.tensor_tensor(rstd[:, :], rstd[:, :], mhalf[:, :], ALU.pow).then_inc(s_rstd, 1)
                    pool.wait_ge(s_rstd, n)
                    pool.sem_inc(passed, 1)
                    hp = h[:, bass.ds(pair * 4, 4), :]
                    pool.tensor_tensor(xc[:, :, :], hp, mv[:, :, 0:1].to_broadcast([R, 4, D]), ALU.subtract).then_inc(s_centred, 1)
                    dst_free()
                    pool.wait_ge(s_centred, n)
                    pool.tensor_tensor(dst, xc[:, :, :], rstd[:, :].rearrange("p (t a) -> p t a", a=1).to_broadcast([R, 4, D]), ALU.mult).then_inc(s_out, 1)
                    pool.tensor_tensor(hp, hp, bias_row[:, :].rearrange("p (a d) -> p a d", a=1).to_broadcast([R, 4, D]), ALU.add).then_inc(s_bias, 1)

                with pool.Fori(0, DEPTH) as l:
                    pool.wait_ge(weights_ready, l + 1)

                    def body(k, b, on):
                        it = l * PAIRS + k
                        if "project" in on:
                            for i in range(2):
                                n = it * 2 + (6 + i)
                                pool.wait_ge(part2, n + 1)
                                pool.tensor_tensor(parts[:, i, 2, :], rest[:, i, :], parts[:, i, 1, :], ALU.subtract).then_inc(parts_ready, 1)
                        if "norm" in on:
                            n = it + 4

                            def y_free():
                                pool.wait_ge(yT_ps, n)
                            normalise(k + 4, n + 1, ln_aggr, ln_var, ln_rstd, ln_centred, y_ready, hbias, y[:, :, :], y_free, bproj)
                    slots(pool, l, body)

                    def mlp(p, b):
                        n = l * PAIRS + p

                        def z_free():
                            if type(p) is not int or p >= NZ:
                                pool.wait_ge(zT_ps, n - (NZ - 1))
                        normalise(p, n + 1, ln2_aggr, ln2_var, ln2_rstd, ln2_centred, z_ready, hbias2, z[:, b, :, :], z_free, bfc2)
                    for p in range(NZ):
                        mlp(p, p)
                    with pool.Fori(0, PAIRS // NZ - 1) as q:
                        for u in range(NZ):
                            mlp(q * NZ + (NZ + u), u)

            RAW = 15 * 16

            @block.scalar
            def _(act):
                act.wait_ge(consts, 2)
                with act.Fori(0, DEPTH) as l:
                    act.wait_ge(weights_ready, l + 1)

                    def body(k, b, on):
                        it = l * PAIRS + k
                        b3 = (b + 3) % NB

                        def exps(g):
                            if "now" not in on:
                                return
                            n = it * (2 * HEADS)
                            if g % 4 == 0 and (type(k) is not int or k > 0 or g >= NP):
                                act.wait_ge(probs_used, it * 4 + (g // 4 - 1))
                            act.wait_ge(st_ps, n + (g + 1))
                            act.activation(probs[:, g % NP, :], ps[0:R, bank_T(b, g)[0], 0:2 * W], ACT.Exp, scale=SCALE).then_inc(probs_ready, 1)

                        def max_high(im, pair, stage):
                            if stage in on:
                                n = pair * 2 + im
                                act.wait_ge(mT_ps, n + 1)
                                act.wait_ge(max_loaded[im], pair * 64)
                                act.activation(mhi[:, im, :], ps[0:2 * HEADS, 7, 0:R], ACT.Copy).then_inc(mhi_ready, 1)

                        def part_one(i):
                            if "project" in on:
                                n = it + 3
                                act.wait_ge(qk_ps, n * 2 + (i + 1))
                                act.wait_ge(qk_saved[i], n * (48, 16)[i])
                                act.activation(parts[:, i, 0, :], ps[:, 7, 0:W2], ACT.Identity, bias=bqkv[:, i:i + 1]).then_inc(part1, 1)

                        def part_two(i):
                            if "project" in on:
                                act.wait_ge(rest_ready, it * 2 + (6 + i + 1))
                                act.activation(parts[:, i, 1, :], rest[:, i, :], ACT.Copy).then_inc(part2, 1)

                        def output(im, pair, stage):
                            if stage in on:
                                n = pair * 2 + im
                                act.wait_ge(oU_turned, n)
                                act.wait_ge(probs_used, pair * 4 + (2 * im + 2))
                                act.activation(oU[:, :], ps[:, 6, 0:2 * W], ACT.Copy).then_inc(oU_ready, 1)

                        def out_T(im, pair, stage):
                            if stage in on:
                                n = pair * 2 + im
                                act.wait_ge(oT_ps, n + 1)
                                act.wait_ge(proj_ps, n)
                                act.activation(oT[:, :], ps[:, 7, 0:W], ACT.Copy).then_inc(oT_ready, 1)

                        for s in range(2 * HEADS):
                            if s == 1:
                                out_T(0, it - 1, "tail")
                            if s == 2:
                                max_high(1, it, "now")
                            if s == 4:
                                output(1, it - 1, "tail")
                            if s == 4 and "project" in on:
                                act.wait_ge(yT_ps, it + 4)
                                act.wait_ge(v_ps, it + 3)
                                act.activation(yT[:, :], ps[:, 7, 0:W2], ACT.Copy).then_inc(yT_ready, 1)
                            if s == 6:
                                part_one(0)
                            if s == 8:
                                part_two(0)
                            if s == 9:
                                part_one(1)
                            if s == 10:
                                out_T(1, it - 1, "tail")
                            if s == 11:
                                max_high(0, it + 1, "maxima")
                                part_two(1)
                            if s == 12:
                                output(0, it, "now")
                            if s == 15 and "project" in on:
                                act.wait_ge(v_ps, it + 4)
                                if "tail" in on:
                                    act.wait_ge(probs_used, it * 4)
                                act.activation(V[:, b3, :, :, 0:HD], ps[0:R, 7, :].rearrange("p (t h d) -> p t h d", t=4, h=HEADS),
                                               ACT.Copy).then_inc(v_ready, 1)
                            exps(s)
                    slots(act, l, body)

                    def transposed(p, b):
                        n = l * PAIRS + p
                        act.wait_ge(zT_ps, n + 1)
                        if type(p) is not int or p >= 2:
                            act.wait_ge(hid_ps, n - 1)
                        act.activation(zT[:, b, :], ps[:, b, 0:W2], ACT.Copy).then_inc(zT_ready, 1)

                    def gelu(p, b):
                        n = l * PAIRS + p
                        act.wait_ge(hid_ps, n + 1)
                        if type(p) is not int or p >= 2:
                            act.wait_ge(fc2_ps, n - 1)
                        for c in range(2):
                            last = act.activation(hid[:, b, c, :], ps[:, 2 + 2 * b + c, 0:W2], ACT.Gelu, bias=bfc1[:, c:c + 1])
                        last.then_inc(hid_ready, 1)

                    transposed(0, 0)
                    transposed(1, 1)
                    gelu(0, 0)
                    with act.Fori(0, (PAIRS - 2) // 2) as q:
                        for u in range(2):
                            transposed(q * 2 + (2 + u), u)
                            gelu(q * 2 + (1 + u), 1 - u)
                    gelu(PAIRS - 1, 1)

            @block.tensor
            def _(pe):
                with pe.Fori(0, DEPTH) as l:
                    pe.wait_ge(raw_in, (l + 1) * RAW)
                    pe.wait_ge(mlp_done, l * PAIRS)
                    for i in range(3):
                        pe.matmul(ps[:, 0, i:i + 1], wqkv_raw[:, i * D:(i + 1) * D], cols[:, 1:2], start=True, stop=True)
                    for i in range(2):
                        last = pe.matmul(ps[:, 0, 3 + i:4 + i], wfc1_raw[:, i * D:(i + 1) * D], cols[:, 3:4], start=True, stop=True)
                    last.then_inc(prep_mm, 1)
                    pe.wait_ge(bvw_ready, l + 1)
                    pe.matmul(ps[0:R, 1, 0:D], bv_wide[:, :], wproj_raw[:, :], start=True, stop=False)
                    pe.matmul(ps[0:R, 1, 0:D], ones[0:1, 0:R], rows[:, 0, :], start=False, stop=True)
                    pe.matmul(ps[0:R, 2, 0:D], ones[0:1, 0:R], rows[:, 1, :], start=True, stop=True).then_inc(prep_mm, 1)
                    pe.wait_ge(weights_ready, l + 1)

                    def body(k, b, on):
                        it = l * PAIRS + k
                        b1, b3 = (b + 1) % NB, (b + 3) % NB

                        def freed(use, pair):
                            kind, im = use.rstrip("01"), int(use[-1]) if use[-1] in "01" else 0
                            s, per, at = {"yT": (yT_ready, 1, 0), "v": (v_ready, 1, 0), "mT": (mlo_ready, 2, im),
                                          "q": (rest_ready, 2, 0), "k": (rest_ready, 2, 1), "oT": (oT_ready, 2, im),
                                          "proj": (attn_done, 2, im)}[kind]
                            pe.wait_ge(s, pair * per + (at + 1))

                        def bank(use):
                            names = [u for u, _ in MISC]
                            i = names.index(use)
                            if MISC[i][1] not in on:
                                return False
                            before = [u for u in MISC[:i] if u[1] in on]
                            if before:
                                freed(before[-1][0], it + LEAD[before[-1][1]])
                            elif type(k) is not int or k >= 1:
                                freed("oT0", it - 1)
                            elif k >= -2:
                                freed("v", it + 2)
                            return True

                        def scores_T(s):
                            im, hd = s // HEADS, s % HEADS
                            bank, before = bank_T(b, s)
                            if type(k) is not int or k > 0 or s >= before:
                                pe.wait_ge(probs_ready, it * (2 * HEADS) + (s - before + 1))
                            if hd == 0:
                                pe.wait_ge(max_loaded[im], it * 64 + 64)
                            for t in range(2):
                                last = pe.matmul(ps[0:R, bank, t * W:(t + 1) * W], K[0:98, b, hd, im * W + t * R:im * W + (t + 1) * R],
                                                 Q[0:98, b, hd, im * W:(im + 1) * W], start=True, stop=True)
                            last.then_inc(st_ps, 1)

                        def scores(s):
                            im, hd = s // HEADS, s % HEADS
                            if s == 0:
                                pe.wait_ge(qk_loaded, it * 144 + 288)
                            if type(k) is not int or k > -1 or s >= 2:
                                pe.wait_ge(mx_done, it * 16 + (16 + s - 1))
                            for t in range(2):
                                last = pe.matmul(ps[0:R, 4 + s % 2, t * W:(t + 1) * W], Q[0:96, b1, hd, im * W + t * R:im * W + (t + 1) * R],
                                                 K[0:96, b1, hd, im * W:(im + 1) * W], start=True, stop=True)
                            last.then_inc(mx_ps, 1)

                        def values(g, pair, bv):
                            im, c = g // 2, g % 2
                            if g == 0:
                                pe.wait_ge(v_ready, pair + 1)
                            if c == 0:
                                pe.wait_ge(oU_ready, pair * 2 + im)
                            pe.wait_ge(probs_ready, pair * (2 * HEADS) + 4 * (g + 1))
                            for tk, rows_k in ((0, R), (1, P1)):
                                for i in range(4):
                                    hd = 4 * c + i
                                    last = pe.matmul(ps[32 * i:32 * i + 32, 6, c * W:(c + 1) * W], V[0:rows_k, bv, im * 2 + tk, hd, :],
                                                     probs[0:rows_k, (4 * g + i) % NP, tk * W:(tk + 1) * W], start=(tk == 0), stop=(tk == 1))
                            last.then_inc(probs_used, 1)

                        def turn(im, pair):
                            pe.wait_ge(oU_ready, pair * 2 + (im + 1))
                            pe.wait_ge(o_ready, pair * 2 + im)
                            for t in range(2):
                                for c in range(2):
                                    last = pe.transpose(ps[0:R, 3, (2 * t + c) * 128:(2 * t + c + 1) * 128], oU[:, c * W + t * R:c * W + (t + 1) * R], ident[:, :])
                            last.then_inc(oU_turned, 1)

                        def max_T(im, pair):
                            pe.wait_ge(mx_done, pair * 16 + (im + 1) * HEADS)
                            pe.transpose(ps[0:2 * HEADS, 7, 0:R], negmax[:, im, :, :].rearrange("p t h -> p (t h)"), ident[0:R, 0:R]).then_inc(mT_ps, 1)

                        def out_T(im, pair):
                            pe.wait_ge(o_ready, pair * 2 + (im + 1))
                            for t in range(2):
                                last = pe.transpose(ps[:, 7, t * R:(t + 1) * R], o[:, t, :], ident[0:R, 0:R])
                            last.then_inc(oT_ps, 1)

                        def proj(im, pair):
                            pe.wait_ge(oT_ready, pair * 2 + (im + 1))
                            for t in range(2):
                                last = pe.matmul(ps[0:R, 7, t * D:(t + 1) * D], oT[:, t * R:(t + 1) * R], wproj[:, :], start=True, stop=True)
                            last.then_inc(proj_ps, 1)

                        for s in range(2 * HEADS):
                            if "now" in on:
                                scores_T(s)
                            if "maxima" in on:
                                scores(s)
                            if s in (6, 10, 14) and "now" in on:
                                values(s // 4 - 1, it, b)
                            if s == 2 and "tail" in on:
                                values(3, it - 1, b3)
                            if s == 5 and "tail" in on:
                                turn(1, it - 1)
                            if s == 13 and "now" in on:
                                turn(0, it)
                            if s == 1 and bank("mT1"):
                                max_T(1, it)
                            if s == 2 and bank("proj0"):
                                proj(0, it - 1)
                            if s == 3 and bank("yT"):
                                pe.wait_ge(y_ready, it + 4)
                                for t in range(4):
                                    last = pe.transpose(ps[:, 7, t * R:(t + 1) * R], y[:, t, :], ident[0:R, 0:R])
                                last.then_inc(yT_ps, 1)
                            if s in (5, 8) and bank("q" if s == 5 else "k"):
                                i = 0 if s == 5 else 1
                                pe.wait_ge(yT_ready, it + 4)
                                pe.matmul(ps[:, 7, 0:W2], wqkv[:, i * D:(i + 1) * D], yT[:, :], start=True, stop=True).then_inc(qk_ps, 1)
                            if s == 9 and bank("oT1"):
                                out_T(1, it - 1)
                            if s == 10 and bank("mT0"):
                                max_T(0, it + 1)
                            if s == 11 and bank("proj1"):
                                proj(1, it - 1)
                            if s == 13 and bank("v"):
                                for t in range(4):
                                    last = pe.matmul(ps[0:R, 7, t * D:(t + 1) * D], yT[:, t * R:(t + 1) * R], wqkv[:, 2 * D:3 * D], start=True, stop=True)
                                last.then_inc(v_ps, 1)
                            if s == 15 and bank("oT0"):
                                out_T(0, it)
                    slots(pe, l, body)

                    def transposes(p, b):
                        n = l * PAIRS + p
                        pe.wait_ge(z_ready, n + 1)
                        if type(p) is not int or p >= 2:
                            pe.wait_ge(zT_ready, n - 1)
                        for t in range(4):
                            last = pe.transpose(ps[:, b % 2, t * R:(t + 1) * R], z[:, b, t, :], ident[0:R, 0:R])
                        last.then_inc(zT_ps, 1)

                    def up(p, b):
                        n = l * PAIRS + p
                        pe.wait_ge(zT_ready, n + 1)
                        if type(p) is not int or p >= 2:
                            pe.wait_ge(hid_ready, n - 1)
                        for c in range(2):
                            last = pe.matmul(ps[:, 2 + 2 * b + c, 0:W2], wfc1[:, c * D:(c + 1) * D], zT[:, b, :], start=True, stop=True)
                        last.then_inc(hid_ps, 1)

                    def down(p, b):
                        n = l * PAIRS + p
                        pe.wait_ge(hid_ready, n + 1)
                        if type(p) is not int or p >= 2:
                            pe.wait_ge(mlp_done, n - 1)
                        else:
                            pe.wait_ge(attn_done, l * (2 * PAIRS) + 2 * PAIRS)
                        for t in range(4):
                            for c in range(2):
                                last = pe.matmul(ps[0:R, 6 + b, t * D:(t + 1) * D], hid[:, b, c, t * R:(t + 1) * R], wfc2[:, c, :],
                                                 start=(c == 0), stop=(c == 1))
                        last.then_inc(fc2_ps, 1)

                    transposes(0, 0)
                    transposes(1, 1)
                    up(0, 0)

                    def four(q):
                        for u in range(4):
                            transposes(q * 4 + (2 + u), (2 + u) % 4)
                            up(q * 4 + (1 + u), (1 + u) % 2)
                            down(q * 4 + u, u % 2)
                    four(0)
                    with pe.Fori(0, PAIRS // 4 - 2) as q:
                        four(q + 1)
                    for p in range(PAIRS - 4, PAIRS):
                        if p + 2 < PAIRS:
                            transposes(p + 2, (p + 2) % 4)
                        if p + 1 < PAIRS:
                            up(p + 1, (p + 1) % 2)
                        down(p, p % 2)

            @block.vector
            def _(dve):
                def statistics(pair, n, s_stats, s_aggr, s_centred):
                    dve.wait_ge(s_centred, n)
                    dve.sem_inc(passed, 1)
                    for t in range(4):
                        last = dve.bn_stats(stats[:, t, :], h[:, bass.ds(pair * 4 + t, 1), :].rearrange("p a d -> p (a d)"))
                    last.then_inc(s_stats, 1)

                def aggregate(n, s_stats, s_aggr):
                    dve.wait_ge(s_stats, n + 1)
                    dve.sem_inc(passed, 1)
                    for t in range(4):
                        last = dve.bn_aggr(mv[:, t, :], stats[:, t, :])
                    last.then_inc(s_aggr, 1)

                with dve.Fori(0, DEPTH) as l:
                    dve.wait_ge(raw_in, (l + 1) * RAW)
                    dve.wait_ge(fc2_ps, l * PAIRS)
                    dve.wait_ge(hbias2, l * PAIRS)
                    dve.wait_ge(mlp_done, l * PAIRS)
                    dve.tensor_scalar(wqkv[:, :], wqkv_raw[:, :], cols[:, 0:1], None, ALU.mult)
                    dve.tensor_scalar(wfc1[:, :], wfc1_raw[:, :], cols[:, 2:3], None, ALU.mult)
                    dve.tensor_copy(wproj[:, :], wproj_raw[:, :])
                    dve.tensor_copy(wfc2[:, :, :], wfc2_raw[:, :, :])
                    dve.wait_ge(prep_mm, l * 2 + 1)
                    dve.tensor_tensor(bfc1[:, :], ps[:, 0, 3:5], fc1b[:, :], ALU.add)
                    dve.tensor_tensor(bqkv[:, :], ps[:, 0, 0:3], qkvb[:, :], ALU.add).then_inc(bias_ready, 1)
                    dve.wait_ge(bias_ready, l + 1)
                    dve.tensor_copy(bv_wide[:, :], bqkv[:, 2:3].to_broadcast([128, R])).then_inc(bvw_ready, 1)
                    dve.wait_ge(prep_mm, l * 2 + 2)
                    dve.tensor_copy(bfc2[:, :], ps[0:R, 2, 0:D])
                    dve.tensor_copy(bproj[:, :], ps[0:R, 1, 0:D]).then_inc(weights_ready, 1)

                    def body(k, b, on):
                        it = l * PAIRS + k

                        def row_max(s):
                            if "maxima" not in on:
                                return
                            im, hd = s // HEADS, s % HEADS
                            n = it + 1
                            dve.wait_ge(mx_ps, n * 16 + (s + 1))
                            if hd == 0 and (type(k) is not int or k > -1):
                                dve.wait_ge(mT_ps, n * 2 + (im - 1))
                            dve.tensor_reduce(negmax[:, im, :, hd], ps[0:R, 4 + s % 2, 0:2 * W].rearrange("p (t c) -> p t c", t=2),
                                              AX.X, ALU.max, negate=True).then_inc(mx_done, 1)

                        def max_low(im, pair, stage):
                            if stage in on:
                                n = pair * 2 + im
                                dve.wait_ge(mhi_ready, n + 1)
                                dve.tensor_tensor(mlo[:, im, :], ps[0:2 * HEADS, 7, 0:R], mhi[:, im, :], ALU.subtract).then_inc(mlo_ready, 1)

                        def remainder(i):
                            if "project" in on:
                                dve.wait_ge(part1, it * 2 + (6 + i + 1))
                                dve.scalar_tensor_tensor(rest[:, i, :], ps[:, 7, 0:W2], bqkv[:, i:i + 1], parts[:, i, 0, :],
                                                         ALU.add, ALU.subtract).then_inc(rest_ready, 1)

                        def normalise(im, pair, stage):
                            if stage in on:
                                n = pair * 2 + im
                                dve.wait_ge(oU_turned, n + 1)
                                heads = ps[0:R, 3, :].rearrange("p (h v) -> p h v", v=32)
                                dve.reciprocal(rsum[:, :], heads[:, :, HD]).then_inc(rsum_ready, 1)
                                dve.wait_ge(oT_ps, n)
                                dve.wait_ge(rsum_ready, n + 1)
                                dve.tensor_tensor(o[:, :, :].rearrange("p t (h d) -> p (t h) d", h=HEADS), heads[:, :, 0:HD],
                                                  rsum[:, :].rearrange("p (h a) -> p h a", a=1).to_broadcast([R, 2 * HEADS, HD]),
                                                  ALU.mult).then_inc(o_ready, 1)

                        def residual(im, pair, pair_in_layer, stage):
                            if stage in on:
                                dve.wait_ge(proj_ps, pair * 2 + (im + 1))
                                dve.wait_ge(hbias, pair + 1)
                                hi = h[:, bass.ds(pair_in_layer * 4 + 2 * im, 2), :]
                                dve.tensor_tensor(hi, ps[0:R, 7, 0:2 * D].rearrange("p (t d) -> p t d", t=2), hi, ALU.add).then_inc(attn_done, 1)

                        for s in range(2 * HEADS):
                            row_max(s)
                            if s == 2:
                                max_low(1, it, "now")
                            if s == 3:
                                residual(0, it - 1, k - 1, "tail")
                            if s == 6:
                                remainder(0)
                            if s == 7:
                                normalise(1, it - 1, "tail")
                            if s == 8 and "norm" in on:
                                statistics(k + 4, it + 4, ln_stats, ln_aggr, ln_centred)
                            if s == 9:
                                remainder(1)
                            if s == 10 and "norm" in on:
                                aggregate(it + 4, ln_stats, ln_aggr)
                            if s == 11:
                                max_low(0, it + 1, "maxima")
                            if s == 12:
                                residual(1, it - 1, k - 1, "tail")
                            if s == 14:
                                normalise(0, it, "now")
                    slots(dve, l, body)

                    def mlp_residual(p, b):
                        n = l * PAIRS + p
                        dve.wait_ge(fc2_ps, n + 1)
                        dve.wait_ge(hbias2, n + 1)
                        hp = h[:, bass.ds(p * 4, 4), :]
                        dve.tensor_tensor(hp, ps[0:R, 6 + b, :].rearrange("p (t d) -> p t d", t=4), hp, ALU.add).then_inc(mlp_done, 1)

                    def mlp_statistics(p):
                        n = l * PAIRS + p
                        dve.wait_ge(attn_done, n * 2 + 2)
                        statistics(p, n, ln2_stats, ln2_aggr, ln2_centred)
                        aggregate(n, ln2_stats, ln2_aggr)

                    for p in range(NZ):
                        mlp_statistics(p)
                    with dve.Fori(0, (PAIRS - NZ) // 2) as q:
                        for u in range(2):
                            mlp_residual(q * 2 + u, u)
                            mlp_statistics(q * 2 + (NZ + u))
                    for p in range(PAIRS - NZ, PAIRS):
                        mlp_residual(p, p % 2)

        EXPERTS = A["Wr"].shape[1]
        GW = D + EXPERTS
        table = nc.dram_tensor("table", [IMAGES, NTOK, GW], f32, kind="Internal").ap()
        sb, pb, sem = scope_tools(top)
        logits = sb("logits", [R, TILES, EXPERTS])
        with ExitStack() as st:
            sb, pb, sem = scope_tools(st)
            UW = D + 1
            NB = 4
            neghalf = sb("r_neghalf", [128, 128])
            eps_t = sb("r_eps_t", [R, 4])
            mhalf = sb("r_mhalf", [R, 4])
            wnorm = sb("r_wnorm", [R, D])
            bnorm = sb("r_bnorm", [R, D])
            wr = sb("r_wr", [128, EXPERTS])
            stats = sb("r_stats", [R, 3, 4, 6])
            mv = sb("r_mv", [R, 3, 4, 2])
            rstd = sb("r_rstd", [R, 3, 4])
            xc = sb("r_xc", [R, 3, 4, D])
            yn = sb("r_yn", [R, 2, 4, D])
            u = sb("r_u", [R, NB, 4, UW])
            square = sb("r_square", [R, 4, D])
            sqsum = sb("r_sqsum", [R, NB, 4])
            nsq = sb("r_nsq", [R, NB, 4])
            uT = sb("r_uT", [128, 2, W2])
            uT2 = sb("r_uT2", [128, 2, W2])
            dist = sb("r_dist", [R, 2, 2, W])
            kern = sb("r_kern", [R, 2, 2 * W])
            prob = sb("r_prob", [R, 2, 2, 2 * W])
            rden = sb("r_rden", [R, 4])
            g = sb("r_g", [R, 2, 4, D])
            gT = sb("r_gT", [128, W2])
            ps = pb("r_ps", [128, 8, 512])

            (consts, rows_in, st_ready, mv_ready, var_ready, rstd_ready, centred) = (
                sem("r_consts"), sem("r_rows_in"), [sem(f"r_st_ready{i}") for i in range(3)], [sem(f"r_mv_ready{i}") for i in range(3)],
                [sem(f"r_var_ready{i}") for i in range(3)], [sem(f"r_rstd_ready{i}") for i in range(3)], [sem(f"r_centred{i}") for i in range(3)])
            scaled, weighted, normed, u_ready, sq_ready, nsq_ready = (sem("r_" + n) for n in (
                "scaled", "weighted", "normed", "u_ready", "sq_ready", "nsq_ready"))
            uT_ps, uT_ready, uT2_ready, dots_ps, dist_ready, kern_ready, prob_ready, attn_ps, rden_ready, h_done = (sem("r_" + n) for n in (
                "uT_ps", "uT_ready", "uT2_ready", "dots_ps", "dist_ready", "kern_ready", "prob_ready", "attn_ps", "rden_ready", "h_done"))
            g_ready, gT_ps, gT_ready, logit_ps, logit_done, h_saved = (sem("r_" + n) for n in (
                "g_ready", "gT_ps", "gT_ready", "logit_ps", "logit_done", "h_saved"))
            g_saved = [sem("r_g_saved0"), sem("r_g_saved1")]
            block = st.enter_context(nc.Block())

            LAGS = {"norm": 5, "unit": 4, "turn": 3, "kernel": 2, "mix": 1, "final": 0, "route": -1}

            def slots(engine, body):
                def on(k):
                    return {n for n, lag in LAGS.items() if 0 <= k + lag < PAIRS}
                for k in range(-5, 1):
                    body(k, k % 4, on(k))
                loops = (PAIRS - 6) // 4
                with engine.Fori(0, loops) as q:
                    for j in range(4):
                        body(q * 4 + (j + 1), (j + 1) % 4, on(1))
                for k in range(loops * 4 + 1, PAIRS + 1):
                    body(k, k % 4, on(k))

            @block.sync
            def _(sp):
                sp.dma_start(wnorm[:, :], A["norm_w"].partition_broadcast(R)).then_inc(rows_in, 16)
                sp.dma_start(bnorm[:, :], A["norm_b"].partition_broadcast(R)).then_inc(rows_in, 16)
                sp.dma_start(wr[:, :], A["Wr"]).then_inc(rows_in, 16)

                def body(k, j, on):
                    if "mix" in on:
                        sp.wait_ge(h_done, k + 2)
                        for im in range(2):
                            save(out[bass.ds(k * 2 + (2 + im), 1)], h[:, bass.ds(k * 4 + (4 + 2 * im), 2), :], h_saved)
                    if "final" in on:
                        sp.wait_ge(g_ready, k + 1)
                        for im in range(2):
                            save(table[bass.ds(k * 2 + im, 1), :, 0:D], g[:, j % 2, 2 * im:2 * im + 2, :], g_saved[j % 2])

                def save(dst, src, s):
                    sp.dma_start(dst[0, 1:NTOK, :].rearrange("(t p) d -> p t d", p=P1), src[0:P1, :, :]).then_inc(s, 16)
                    sp.dma_start(dst[0, 0:1, :], src[P1:R, 0, :]).then_inc(s, 16)
                slots(sp, body)
                sp.wait_ge(h_saved, IMAGES * 32)
                for i in range(2):
                    sp.wait_ge(g_saved[i], IMAGES * 16)

            @block.gpsimd
            def _(pool):
                pool.memset(neghalf[:, :], -0.5)
                pool.memset(eps_t[:, :], EPS)
                pool.memset(mhalf[:, :], -0.5)
                pool.memset(u[:, :, :, :], 1.0).then_inc(consts, 1)
                pool.wait_ge(consts, 1)
                pool.wait_ge(rows_in, 48)

                def wide(row):
                    return row[:, :].rearrange("p (a d) -> p a d", a=1).to_broadcast([R, 4, D])

                def centre(i, n, pair):
                    pool.wait_ge(mv_ready[i], n)
                    pool.tensor_tensor(rstd[:, i, :], mv[:, i, :, 1], eps_t[:, :], ALU.add).then_inc(var_ready[i], 1)
                    pool.wait_ge(var_ready[i], n)
                    pool.tensor_tensor(rstd[:, i, :], rstd[:, i, :], mhalf[:, :], ALU.pow).then_inc(rstd_ready[i], 1)
                    pool.wait_ge(rstd_ready[i], n)
                    pool.sem_inc(passed, 1)
                    pool.tensor_tensor(xc[:, i, :, :], h[:, bass.ds(pair * 4, 4), :], mv[:, i, :, 0:1].to_broadcast([R, 4, D]),
                                       ALU.subtract).then_inc(centred[i], 1)
                    pool.wait_ge(centred[i], n)

                def spread(i):
                    return rstd[:, i, :].rearrange("p (t a) -> p t a", a=1).to_broadcast([R, 4, D])

                def body(k, j, on):
                    if "final" in on:
                        if type(k) is not int or k > 0:
                            pool.wait_ge(g_ready, k)
                        centre(2, k + 1, k)
                        if type(k) is not int or k >= 2:
                            pool.wait_ge(g_saved[j % 2], (k - j % 2) * 32)
                        if type(k) is not int or k >= 2:
                            pool.wait_ge(gT_ps, k - 1)
                        pool.tensor_tensor(g[:, j % 2, :, :], xc[:, 2, :, :], spread(2), ALU.mult).then_inc(g_ready, 1)
                    if "unit" in on:
                        n = k + 4
                        if type(k) is not int or n > 0:
                            pool.wait_ge(u_ready, n)
                        centre(1, n + 1, n)
                        if type(k) is not int or k >= 0:
                            pool.wait_ge(attn_ps, k * 2 + 2)
                        pool.tensor_tensor(u[:, j, :, 0:D], xc[:, 1, :, :], spread(1), ALU.mult).then_inc(u_ready, 1)
                    if "norm" in on:
                        n = k + 5
                        if type(k) is not int or n > 0:
                            pool.wait_ge(normed, n)
                        centre(0, n + 1, n)
                        pool.tensor_tensor(yn[:, 0, :, :], xc[:, 0, :, :], spread(0), ALU.mult).then_inc(scaled, 1)
                        pool.wait_ge(scaled, n + 1)
                        pool.tensor_tensor(yn[:, 1, :, :], yn[:, 0, :, :], wide(wnorm), ALU.mult).then_inc(weighted, 1)
                        pool.wait_ge(weighted, n + 1)
                        pool.sem_inc(passed, 1)
                        pool.tensor_tensor(h[:, bass.ds(n * 4, 4), :], yn[:, 1, :, :], wide(bnorm), ALU.add).then_inc(normed, 1)
                    if "unit" in on:
                        n = k + 4
                        pool.wait_ge(sq_ready, n + 1)
                        pool.tensor_tensor(nsq[:, j, :], sqsum[:, j, :], mhalf[:, :], ALU.mult).then_inc(nsq_ready, 1)
                slots(pool, body)

            @block.scalar
            def _(act):
                def body(k, j, on):
                    if "route" in on:
                        act.wait_ge(gT_ps, k)
                        act.wait_ge(logit_ps, k - 1)
                        act.activation(gT[:, :], ps[:, 6, 0:W2], ACT.Copy).then_inc(gT_ready, 1)
                    if "turn" in on:
                        n = k + 3
                        act.wait_ge(uT_ps, n + 1)
                        if type(k) is not int or k >= -1:
                            act.wait_ge(dots_ps, k * 2 + 4)
                        act.activation(uT[:, (j + 1) % 2, :], ps[:, 0, 0:W2], ACT.Copy).then_inc(uT_ready, 1)
                        act.activation(uT2[:, (j + 1) % 2, :], ps[:, 0, 0:W2], ACT.Square).then_inc(uT2_ready, 1)
                    if "kernel" in on:
                        for im in range(2):
                            n = k * 2 + (4 + im)
                            act.wait_ge(dist_ready, n + 1)
                            if type(k) is not int or k > -2:
                                act.wait_ge(prob_ready, n - 1)
                            act.activation(kern[:, im, :], dist[:, im, :, :].rearrange("p t c -> p (t c)"), ACT.Exp, scale=2.0).then_inc(kern_ready, 1)
                            act.wait_ge(kern_ready, n + 1)
                            if type(k) is not int or k >= 0:
                                act.wait_ge(attn_ps, n - 3)
                            act.activation(prob[:, j % 2, im, :], kern[:, im, :], ACT.Exp).then_inc(prob_ready, 1)
                    if "unit" in on:
                        n = k + 4
                        act.wait_ge(u_ready, n + 1)
                        if type(k) is not int or k >= -1:
                            act.wait_ge(nsq_ready, n - 3)
                        if type(k) is not int or k > -4:
                            act.wait_ge(sq_ready, n)
                        for t in range(4):
                            last = act.activation(square[:, t, :], u[:, j, t, 0:D], ACT.Square, accum_out=sqsum[:, j, t:t + 1])
                        last.then_inc(sq_ready, 1)
                slots(act, body)

            @block.tensor
            def _(pe):
                pe.wait_ge(consts, 1)
                pe.wait_ge(rows_in, 48)

                def body(k, j, on):
                    if "route" in on:
                        pe.wait_ge(g_ready, k)
                        pe.wait_ge(gT_ready, k - 1)
                        for t in range(4):
                            last = pe.transpose(ps[:, 6, t * R:(t + 1) * R], g[:, (j + 1) % 2, t, :], ident[0:R, 0:R])
                        last.then_inc(gT_ps, 1)
                    if "turn" in on:
                        n = k + 3
                        pe.wait_ge(u_ready, n + 1)
                        pe.wait_ge(uT2_ready, n)
                        for t in range(4):
                            last = pe.transpose(ps[:, 0, t * R:(t + 1) * R], u[:, (j + 3) % 4, t, 0:D], ident[0:R, 0:R])
                        last.then_inc(uT_ps, 1)
                    if "kernel" in on:
                        n = k + 2
                        b = j % 2
                        pe.wait_ge(uT2_ready, n + 1)
                        pe.wait_ge(uT_ready, n + 1)
                        for im in range(2):
                            if type(k) is not int or k > -2:
                                pe.wait_ge(dist_ready, n * 2 + (im - 1))
                            for t in range(2):
                                dst = ps[0:R, 2 + im, t * W:(t + 1) * W]
                                pe.matmul(dst, uT[:, b, im * W + t * R:im * W + (t + 1) * R], uT[:, b, im * W:(im + 1) * W], start=True, stop=False)
                                last = pe.matmul(dst, neghalf[:, 0:R], uT2[:, b, im * W:(im + 1) * W], start=False, stop=True)
                            last.then_inc(dots_ps, 1)
                    if "mix" in on:
                        n = k + 1
                        for im in range(2):
                            pe.wait_ge(prob_ready, n * 2 + (im + 1))
                            if type(k) is not int or k >= 0:
                                pe.wait_ge(h_done, n)
                            for tq in range(2):
                                for tk, rows_k in ((0, R), (1, P1)):
                                    last = pe.matmul(ps[0:R, 4 + im, tq * UW:(tq + 1) * UW], prob[0:rows_k, (j + 1) % 2, im, tk * W + tq * R:tk * W + (tq + 1) * R],
                                                     u[0:rows_k, (j + 1) % 4, 2 * im + tk, :], start=(tk == 0), stop=(tk == 1))
                            last.then_inc(attn_ps, 1)
                    if "route" in on:
                        pe.wait_ge(gT_ready, k)
                        pe.wait_ge(logit_done, k - 1)
                        for t in range(4):
                            last = pe.matmul(ps[0:R, 7, t * EXPERTS:(t + 1) * EXPERTS], gT[:, t * R:(t + 1) * R], wr[:, :], start=True, stop=True)
                        last.then_inc(logit_ps, 1)
                slots(pe, body)

            @block.vector
            def _(dve):
                dve.wait_ge(consts, 1)

                def statistics(i, n, pair):
                    dve.wait_ge(centred[i], n)
                    dve.sem_inc(passed, 1)
                    for t in range(4):
                        last = dve.bn_stats(stats[:, i, t, :], h[:, bass.ds(pair * 4 + t, 1), :].rearrange("p a d -> p (a d)"))
                    last.then_inc(st_ready[i], 1)
                    dve.wait_ge(st_ready[i], n + 1)
                    dve.sem_inc(passed, 1)
                    for t in range(4):
                        last = dve.bn_aggr(mv[:, i, t, :], stats[:, i, t, :])
                    last.then_inc(mv_ready[i], 1)

                def body(k, j, on):
                    if "mix" in on:
                        n = k + 1
                        for im in range(2):
                            dve.wait_ge(attn_ps, n * 2 + (im + 1))
                            outs = ps[0:R, 4 + im, 0:2 * UW].rearrange("p (t d) -> p t d", t=2)
                            dve.reciprocal(rden[:, 2 * im:2 * im + 2], outs[:, :, D]).then_inc(rden_ready, 1)
                            dve.wait_ge(rden_ready, n * 2 + (im + 1))
                            for t in range(2):
                                hi = h[:, bass.ds(n * 4 + (2 * im + t), 1), :].rearrange("p a d -> p (a d)")
                                last = dve.scalar_tensor_tensor(hi, outs[:, t, 0:D], rden[:, 2 * im + t:2 * im + t + 1], hi, ALU.mult, ALU.add)
                        last.then_inc(h_done, 1)
                    if "kernel" in on:
                        n = k + 2
                        dve.wait_ge(nsq_ready, n + 1)
                        for im in range(2):
                            dve.wait_ge(dots_ps, n * 2 + (im + 1))
                            if type(k) is not int or k > -2:
                                dve.wait_ge(kern_ready, n * 2 + (im - 1))
                            for t in range(2):
                                last = dve.tensor_scalar(dist[:, im, t, :], ps[0:R, 2 + im, t * W:(t + 1) * W],
                                                         nsq[:, (j + 2) % 4, 2 * im + t:2 * im + t + 1], 0.0, ALU.add, ALU.min)
                            last.then_inc(dist_ready, 1)
                    if "norm" in on:
                        statistics(0, k + 5, k + 5)
                    if "unit" in on:
                        dve.wait_ge(normed, k + 5)
                        statistics(1, k + 4, k + 4)
                    if "final" in on:
                        dve.wait_ge(h_done, k + 1)
                        statistics(2, k, k)
                    if "route" in on:
                        dve.wait_ge(logit_ps, k)
                        dve.sem_inc(passed, 1)
                        dve.tensor_copy(logits[:, bass.ds(k * 4 - 4, 4), :], ps[0:R, 7, 0:4 * EXPERTS].rearrange("p (t e) -> p t e", t=4)).then_inc(logit_done, 1)
                slots(dve, body)

        CAP = 1024
        F = A["W1"].shape[2]
        FC = F // 128
        E8 = EXPERTS
        TB = TILES // (128 // E8)
        LO, HI = 64, CAP // 64
        EH = 2
        SL = CAP // 128
        table_rows = table.rearrange("b n w -> (b n) w")
        out_rows = out.rearrange("b n d -> (b n) d")
        sb, pb, sem = scope_tools(top)
        index_all = sb("index_all", [128, E8, SL], i32)
        with ExitStack() as st:
            sb, pb, sem = scope_tools(st)
            dup = sb("dup", [R, 2])
            dup1 = sb("dup1", [R, 2])
            fold = sb("fold", [128, E8])
            same = sb("same", [128, 128])
            before = sb("before", [R, R], bf16)
            onesb = sb("onesb", [R, 128], bf16)
            iota_n = sb("iota_n", [R, 2], i32)
            iota_b = sb("iota_b", [R, IMAGES], i32)
            n_f = sb("n_f", [R, 2])
            nval = sb("nval", [R, IMAGES, 2], bf16)
            bval = sb("bval", [R, IMAGES, 2], bf16)
            colmax = sb("colmax", [128, 1])
            negmax8 = sb("negmax8", [1, E8])
            row = sb("row", [1, 128])
            nmax = sb("nmax", [128, 1])
            esum = sb("esum", [128, 1])
            rsum = sb("rsum8", [128, 1])
            expd = sb("expd", [128, TB * R])
            pT = sb("pT", [128, TB * R])
            over = sb("over", [128, TB * R])
            pm = sb("pm", [R, TILES, E8])
            cand = sb("cand", [128, 1])
            low = sb("low", [128, 1])
            step = sb("step", [128, 1])
            count = sb("count", [128, 1])
            flag = sb("flag", [128, 1])
            row8 = sb("row8", [1, E8])
            thr = sb("thr", [R, E8])
            above = sb("above", [R, TILES, E8], bf16)
            equal = sb("equal", [R, TILES, E8], bf16)
            chosen = sb("chosen", [R, TILES, E8], bf16)
            running = sb("running", [R, TILES, E8])
            rank = sb("rank", [R, TILES, E8])
            taken = sb("taken", [R, E8])
            room = sb("room", [R, E8])
            slot_i = sb("slot_i", [R, TILES, E8], i32)
            slot_h = sb("slot_h", [R, TILES, E8], i32)
            lo_b = sb("lo_b", [R, E8, TILES], bf16)
            hi_b = sb("hi_b", [R, E8, TILES], bf16)
            lo_hot = sb("lo_hot", [R, LO, EH, TILES], bf16)
            hi_hot = sb("hi_hot", [R, HI, EH, TILES], bf16)
            hi_val = sb("hi_val", [R, 2, HI, EH, TILES], bf16)
            tok_b = sb("tok_b", [LO, E8 // EH, EH, HI])
            index = sb("index", [LO, 2, E8, SL], i32)
            ps = pb("moe_ps", [128, 8, 512])
            ps_flat = ps[:, :, :].rearrange("p a b -> p (a b)")

            setup, ready, turned = sem("setup"), sem("ready"), sem("turned")
            dve_n, pe_n, exp_done, p_saved, idx_moved = sem("dve_n"), sem("pe_n"), sem("exp_done"), sem("p_saved"), sem("idx_moved")
            cand_ready, counted, total, flagged, hot_ready, idx_ps, idx_read = (sem(n) for n in (
                "cand_ready", "counted", "total", "flagged", "hot_ready", "idx_ps", "idx_read"))
            block = st.enter_context(nc.Block())

            STEPS = ["masked", "colmax", "negmax", "row", "nmax", "rsum", "pT", "pm_raw", "pm", "low0"]
            AT = {n: i + 1 for i, n in enumerate(STEPS)}

            @block.gpsimd
            def _(pool):
                def put(ins, n):
                    ins.then_inc(setup, 1)
                    pool.wait_ge(setup, n)
                put(pool.memset(dup[:, :], 0.0), 1)
                put(pool.affine_select(out=dup[:, 1:2], in_=dup[:, 1:2], compare_op=ALU.not_equal, fill=-3.0e38, base=-P1,
                                       pattern=[[0, 1]], channel_multiplier=1), 2)
                put(pool.memset(dup1[:, :], 0.0), 3)
                put(pool.affine_select(out=dup1[:, 1:2], in_=dup1[:, 1:2], compare_op=ALU.not_equal, fill=-1.0, base=-P1,
                                       pattern=[[0, 1]], channel_multiplier=1), 4)
                put(pool.memset(onesb[:, :], 1.0), 5)
                put(pool.memset(before[:, 0:P1], 1.0), 6)
                put(pool.memset(before[:, P1:R], 0.0), 7)
                put(pool.affine_select(out=before[:, 0:P1], in_=before[:, 0:P1], compare_op=ALU.is_gt, fill=0.0, base=0,
                                       pattern=[[1, P1]], channel_multiplier=-1), 8)
                put(pool.affine_select(out=before[:, 0:P1], in_=before[:, 0:P1], compare_op=ALU.not_equal, fill=1.0, base=-P1,
                                       pattern=[[0, P1]], channel_multiplier=1), 9)
                put(pool.iota(iota_n[:, :], pattern=[[P1, 2]], base=1, channel_multiplier=1), 10)
                put(pool.iota(iota_b[:, :], pattern=[[1, IMAGES]], base=0, channel_multiplier=0), 11)
                put(pool.tensor_copy(n_f[:, :], iota_n[:, :]), 12)
                put(pool.affine_select(out=n_f[:, :], in_=n_f[:, :], compare_op=ALU.not_equal, fill=0.0, base=-P1,
                                       pattern=[[0, 2]], channel_multiplier=1), 13)
                pool.tensor_copy(nval[:, :, :], n_f[:, :].rearrange("p (a t) -> p a t", a=1).to_broadcast([R, IMAGES, 2])).then_inc(setup, 1)
                pool.tensor_copy(bval[:, :, :], iota_b[:, :].rearrange("p (b a) -> p b a", a=1).to_broadcast([R, IMAGES, 2])).then_inc(setup, 1)
            SETUP = 15

            @block.sync
            def _(sp):
                sp.wait_ge(dve_n, AT["pm"])
                for t in range(2):
                    sp.dma_start(table[:, 1 + t * P1:1 + (t + 1) * P1, D:GW].rearrange("b p e -> p b e"),
                                 pm[0:P1, :, :].rearrange("p (b t) e -> p b t e", t=2)[:, :, t, :]).then_inc(p_saved, 16)
                sp.dma_start(table[:, 0:1, D:GW].rearrange("b p e -> p b e"),
                             pm[P1:R, :, :].rearrange("p (b t) e -> p b t e", t=2)[:, :, 0, :]).then_inc(p_saved, 16)
                sp.wait_ge(idx_read, E8 // EH)
                sp.dma_start(index_all[LO:128, :, :], index[:, 1, :, :]).then_inc(idx_moved, 16)
                sp.wait_ge(idx_moved, 16)
                sp.wait_ge(p_saved, 48)

            @block.scalar
            def _(act):
                act.wait_ge(dve_n, AT["nmax"])
                act.activation(expd[:, :].rearrange("p (a b) -> p a b", a=2), ps[:, 0:2, 0:TB * R // 2], ACT.Exp, bias=nmax[:, 0:1],
                               accum_out=esum[:, 0:1]).then_inc(exp_done, 1)

            MANTISSA = 23

            @block.tensor
            def _(pe):
                pe.wait_ge(dve_n, AT["masked"])
                for i in range(TB):
                    last = pe.transpose(ps[:, i // 4, (i % 4) * R:(i % 4 + 1) * R],
                                        logits[:, 16 * i:16 * (i + 1), :].rearrange("p t e -> p (t e)"), ident[0:R, 0:R])
                last.then_inc(pe_n, 1)
                pe.wait_ge(dve_n, AT["colmax"])
                pe.transpose(ps[0:1, 2, 0:128], colmax[:, 0:1], ident[:, :]).then_inc(pe_n, 1)
                pe.wait_ge(dve_n, AT["row"])
                pe.matmul(ps[:, 3, 0:1], row[0:1, :], ones[0:1, 0:1], start=True, stop=True).then_inc(pe_n, 1)
                pe.wait_ge(exp_done, 1)
                pe.matmul(ps[:, 2, 0:1], same[:, :], esum[:, 0:1], start=True, stop=True).then_inc(pe_n, 1)
                pe.wait_ge(dve_n, AT["pT"])
                for i in range(TB):
                    last = pe.transpose(ps[0:R, 4 + i // 4, (i % 4) * 128:(i % 4 + 1) * 128], pT[:, i * R:(i + 1) * R], ident[:, :])
                last.then_inc(pe_n, 1)

                def sum_up(n):
                    pe.wait_ge(counted, n)
                    pe.matmul(ps[:, 6, 0:1], same[:, :], count[:, 0:1], start=True, stop=True).then_inc(total, 1)
                for n in range(7):
                    sum_up(n + 1)
                with pe.Fori(0, MANTISSA) as i:
                    sum_up(i + 8)
                sum_up(7 + MANTISSA + 1)
                pe.wait_ge(ready, 1)
                pe.transpose(ps[0:1, 7, 0:128], low[:, 0:1], ident[:, :]).then_inc(turned, 1)
                pe.wait_ge(ready, 2)
                pe.matmul(ps[0:R, 6, 0:E8], ones[0:1, 0:R], row8[0:1, :], start=True, stop=True).then_inc(turned, 1)

                def prefix(mask, bank_prefix, bank_total):
                    m = mask[:, :, :].rearrange("p t e -> p (t e)")
                    for i in range(2):
                        if bank_prefix is not None:
                            pe.matmul(ps[0:R, bank_prefix + i, :], before[:, :], m[:, i * 512:(i + 1) * 512], start=True, stop=True)
                        last = pe.matmul(ps[0:R, bank_total + i, :], onesb[:, 0:R], m[:, i * 512:(i + 1) * 512], start=True, stop=True)
                    last.then_inc(turned, 1)
                pe.wait_ge(ready, 3)
                prefix(equal, 0, 2)
                prefix(above, None, 4)
                pe.wait_ge(ready, 4)
                prefix(chosen, 0, 2)
                for c in range(E8 // EH):
                    pe.wait_ge(hot_ready, c + 1)
                    if c == 0:
                        pe.wait_ge(ready, 5)

                    def place(tile, start, stop):
                        for e in range(EH):
                            last = pe.matmul(ps[0:LO, EH * c + e, 0:2 * HI], lo_hot[:, :, e, tile] if start or stop else lo_hot[:, :, e, bass.ds(tile, 1)].rearrange("p l a -> p (l a)"),
                                             hi_val[:, :, :, e, tile] if start or stop else hi_val[:, :, :, e, bass.ds(tile, 1)].rearrange("p v c a -> p v (c a)"),
                                             start=start, stop=stop)
                        return last
                    place(0, True, False)
                    with pe.Fori(1, TILES - 1) as tile:
                        place(tile, False, False)
                    place(TILES - 1, False, True).then_inc(idx_ps, 1)

            @block.vector
            def _(dve):
                def put(ins, n):
                    ins.then_inc(dve_n, 1)
                    dve.wait_ge(dve_n, AT[n])
                dve.wait_ge(setup, SETUP)
                dve.tensor_reduce(fold[:, :], ident[:, :].rearrange("p (i e) -> p e i", e=E8), AX.X, ALU.add)
                put(dve.tensor_tensor(logits[:, :, :].rearrange("p (b t) e -> p b t e", t=2), logits[:, :, :].rearrange("p (b t) e -> p b t e", t=2),
                                      dup[:, :].rearrange("p (a t c) -> p a t c", a=1, c=1).to_broadcast([R, IMAGES, 2, E8]), ALU.add), "masked")
                dve.tensor_copy(same[:, :].rearrange("p (i e) -> p i e", e=E8), fold[:, :].rearrange("p (a e) -> p a e", a=1).to_broadcast([128, 128 // E8, E8]))
                dve.wait_ge(pe_n, 1)
                put(dve.tensor_reduce(colmax[:, :], ps[:, 0:2, 0:TB * R // 2], AX.XY, ALU.max), "colmax")
                dve.wait_ge(pe_n, 2)
                put(dve.tensor_reduce(negmax8[:, :], ps[0:1, 2, 0:128].rearrange("p (i e) -> p e i", e=E8), AX.X, ALU.max, negate=True), "negmax")
                put(dve.tensor_copy(row[:, :].rearrange("p (i e) -> p i e", e=E8), negmax8[:, :].rearrange("p (a e) -> p a e", a=1).to_broadcast([1, 128 // E8, E8])), "row")
                dve.wait_ge(pe_n, 3)
                put(dve.tensor_copy(nmax[:, :], ps[:, 3, 0:1]), "nmax")
                dve.wait_ge(pe_n, 4)
                put(dve.reciprocal(rsum[:, :], ps[:, 2, 0:1]), "rsum")
                put(dve.tensor_scalar(pT[:, :], expd[:, :], rsum[:, 0:1], None, ALU.mult), "pT")
                dve.wait_ge(pe_n, 5)
                put(dve.tensor_copy(pm[:, :, :].rearrange("p t e -> p (t e)"), ps_flat[0:R, 2048:2048 + TILES * E8]), "pm_raw")
                put(dve.tensor_tensor(pm[:, :, :].rearrange("p (b t) e -> p b t e", t=2), pm[:, :, :].rearrange("p (b t) e -> p b t e", t=2),
                                      dup1[:, :].rearrange("p (a t c) -> p a t c", a=1, c=1).to_broadcast([R, IMAGES, 2, E8]), ALU.add), "pm")

                put(dve.memset(low[:, :], 2.0 ** -126), "low0")
                n = 0

                def try_cand(n):
                    dve.wait_ge(cand_ready, n)
                    dve.tensor_scalar(over[:, :], pT[:, :], cand[:, 0:1], None, ALU.is_ge, ALU.add, accum_out=count[:, 0:1]).then_inc(counted, 1)
                for i in range(7):
                    dve.tensor_scalar(cand[:, :], low[:, :], float(2.0 ** (64 >> i)), None, ALU.mult).then_inc(cand_ready, 1)
                    try_cand(i + 1)
                    dve.wait_ge(total, i + 1)
                    dve.tensor_scalar(flag[:, :], ps[:, 6, 0:1], CAP - 0.5, float(2.0 ** (64 >> i)) - 1.0, ALU.is_ge, ALU.mult).then_inc(flagged, 1)
                    dve.wait_ge(flagged, 2 * i + 1)
                    dve.scalar_tensor_tensor(low[:, :], flag[:, :], 1.0, low[:, :], ALU.add, ALU.mult).then_inc(flagged, 1)
                    dve.wait_ge(flagged, 2 * i + 2)
                dve.tensor_scalar(step[:, :], low[:, :], 0.5, None, ALU.mult).then_inc(flagged, 1)
                dve.tensor_scalar(cand[:, :], low[:, :], 1.5, None, ALU.mult).then_inc(cand_ready, 1)
                dve.wait_ge(flagged, 15)
                with dve.Fori(0, MANTISSA - 1) as i:
                    try_cand(i + 8)
                    dve.wait_ge(total, i + 8)
                    dve.tensor_scalar(flag[:, :], ps[:, 6, 0:1], CAP - 0.5, 0.5, ALU.is_ge, ALU.subtract).then_inc(flagged, 1)
                    dve.wait_ge(flagged, i * 2 + 16)
                    dve.scalar_tensor_tensor(cand[:, :], flag[:, :], step[:, 0:1], cand[:, :], ALU.mult, ALU.add).then_inc(cand_ready, 1)
                    dve.wait_ge(cand_ready, i + 9)
                    dve.tensor_scalar(step[:, :], step[:, :], 0.5, None, ALU.mult).then_inc(flagged, 1)
                    dve.wait_ge(flagged, i * 2 + 17)
                try_cand(7 + MANTISSA)
                F0 = 15 + 2 * (MANTISSA - 1)
                dve.wait_ge(total, 7 + MANTISSA)
                dve.tensor_scalar(flag[:, :], ps[:, 6, 0:1], CAP - 0.5, 1.0, ALU.is_ge, ALU.subtract).then_inc(flagged, 1)
                dve.wait_ge(flagged, F0 + 1)
                dve.scalar_tensor_tensor(cand[:, :], flag[:, :], step[:, 0:1], cand[:, :], ALU.mult, ALU.add).then_inc(cand_ready, 1)
                try_cand(8 + MANTISSA)
                dve.wait_ge(total, 8 + MANTISSA)
                dve.tensor_scalar(flag[:, :], ps[:, 6, 0:1], CAP - 0.5, None, ALU.is_ge).then_inc(flagged, 1)
                dve.wait_ge(flagged, F0 + 2)
                dve.tensor_tensor(low[:, :], flag[:, :], cand[:, :], ALU.mult).then_inc(ready, 1)
                dve.wait_ge(turned, 1)
                dve.tensor_copy(row8[:, :], ps[0:1, 7, 0:E8]).then_inc(ready, 1)
                dve.wait_ge(turned, 2)
                dve.tensor_copy(thr[:, :], ps[0:R, 6, 0:E8]).then_inc(flagged, 1)
                dve.wait_ge(flagged, F0 + 3)
                wide_thr = thr[:, :].rearrange("p (a e) -> p a e", a=1).to_broadcast([R, TILES, E8])
                dve.tensor_tensor(above[:, :, :], pm[:, :, :], wide_thr, ALU.is_gt)
                dve.tensor_tensor(equal[:, :, :], pm[:, :, :], wide_thr, ALU.is_equal).then_inc(ready, 1)

                def bank(i):
                    return ps_flat[0:R, i * 512:i * 512 + TILES * E8].rearrange("p (t e) -> p t e", e=E8)

                def ranks(f0):
                    for e in range(E8):
                        last = dve.tensor_tensor_scan(running[:, :, e], ones[0:R, 0:TILES], bank(2)[:, :, e], 0.0, ALU.mult, ALU.add)
                    last.then_inc(flagged, 1)
                    dve.wait_ge(flagged, f0 + 1)
                    dve.tensor_tensor(rank[:, :, :], bank(2), running[:, :, :], ALU.subtract).then_inc(flagged, 1)
                    dve.wait_ge(flagged, f0 + 2)
                    dve.tensor_tensor(rank[:, :, :], bank(0), rank[:, :, :], ALU.subtract).then_inc(flagged, 1)
                    dve.wait_ge(flagged, f0 + 3)

                dve.wait_ge(turned, 4)
                dve.tensor_reduce(taken[:, :], bank(4).rearrange("p t e -> p e t"), AX.X, ALU.add).then_inc(flagged, 1)
                dve.wait_ge(flagged, F0 + 4)
                dve.tensor_scalar(room[:, :], taken[:, :], -1.0, float(CAP), ALU.mult, ALU.add).then_inc(flagged, 1)
                dve.wait_ge(flagged, F0 + 5)
                ranks(F0 + 5)
                dve.tensor_tensor(rank[:, :, :], rank[:, :, :], room[:, :].rearrange("p (a e) -> p a e", a=1).to_broadcast([R, TILES, E8]), ALU.is_lt).then_inc(flagged, 1)
                dve.wait_ge(flagged, F0 + 9)
                dve.tensor_tensor(rank[:, :, :], rank[:, :, :], equal[:, :, :], ALU.mult).then_inc(flagged, 1)
                dve.wait_ge(flagged, F0 + 10)
                dve.tensor_tensor(chosen[:, :, :], rank[:, :, :], above[:, :, :], ALU.add).then_inc(ready, 1)
                dve.wait_ge(turned, 5)
                ranks(F0 + 10)
                dve.tensor_scalar(running[:, :, :], chosen[:, :, :], -4.0 * CAP, 4.0 * CAP, ALU.mult, ALU.add).then_inc(ready, 1)
                dve.wait_ge(ready, 5)
                dve.tensor_tensor(slot_i[:, :, :], rank[:, :, :], running[:, :, :], ALU.add).then_inc(flagged, 1)
                dve.wait_ge(flagged, F0 + 14)
                dve.tensor_scalar(slot_h[:, :, :], slot_i[:, :, :], 6, None, ALU.arith_shift_right).then_inc(flagged, 1)
                dve.wait_ge(flagged, F0 + 15)
                dve.tensor_copy(hi_b[:, :, :].rearrange("p e t -> p t e"), slot_h[:, :, :])
                dve.tensor_scalar(slot_i[:, :, :], slot_i[:, :, :], LO - 1, None, ALU.bitwise_and).then_inc(flagged, 1)
                dve.wait_ge(flagged, F0 + 16)
                dve.tensor_copy(lo_b[:, :, :].rearrange("p e t -> p t e"), slot_i[:, :, :]).then_inc(flagged, 1)
                dve.wait_ge(flagged, F0 + 17)
                for c in range(E8 // EH):
                    ce = slice(c * EH, (c + 1) * EH)
                    if c:
                        dve.wait_ge(idx_ps, c)
                    for i in range(HI):
                        last = dve.tensor_scalar(hi_hot[:, i, :, :], hi_b[:, ce, :], float(i), None, ALU.is_equal)
                    last.then_inc(flagged, 1)
                    for i in range(LO):
                        dve.tensor_scalar(lo_hot[:, i, :, :], lo_b[:, ce, :], float(i), None, ALU.is_equal)
                    dve.wait_ge(flagged, F0 + 18 + c)
                    for v, val in enumerate((nval, bval)):
                        last = dve.tensor_tensor(hi_val[:, v, :, :, :].rearrange("p c e t -> p (c e) t"), hi_hot[:, :, :, :].rearrange("p c e t -> p (c e) t"),
                                                 val[:, :, :].rearrange("p (a b) t -> p a (b t)", a=1).to_broadcast([R, HI * EH, TILES]), ALU.mult)
                    last.then_inc(hot_ready, 1)
                for c in range(E8 // EH):
                    dve.wait_ge(idx_ps, c + 1)
                    both = ps[0:LO, EH * c:EH * c + EH, 0:2 * HI].rearrange("p e (v q r) -> p v e q r", v=2, r=2)
                    tb = tok_b[:, c, :, :].rearrange("p e (q r) -> p e q r", r=2)
                    for r in range(2):
                        dve.tensor_copy(tb[:, :, :, r], both[:, 1, :, :, r]).then_inc(flagged, 1)
                    dve.wait_ge(flagged, F0 + 18 + E8 // EH + 2 * c + 1)
                    for r in range(2):
                        last = dve.scalar_tensor_tensor(index[:, r, c * EH:(c + 1) * EH, :], tb[:, :, :, r], float(NTOK), both[:, 0, :, :, r], ALU.mult, ALU.add)
                    last.then_inc(idx_read, 1)
                dve.wait_ge(idx_read, E8 // EH)
                dve.tensor_copy(index_all[0:LO, :, :], index[:, 0, :, :])

        ffn(nc, A, out_rows, table_rows, index_all, ident, ones, passed)


def ffn(nc, A, out_rows, table_rows, index_all, ident, ones, passed):
    import concourse.bass as bass
    from concourse import mybir
    from contextlib import ExitStack

    f32, i32 = mybir.dt.float32, mybir.dt.int32
    ALU = mybir.AluOpType
    ACT = mybir.ActivationFunctionType
    EXPERTS, D, F = A["W1"].shape
    FC = F // 128
    SL = index_all.shape[2]
    GW = table_rows.shape[1]
    with ExitStack() as st:
        def sb(name, shape, dt=f32):
            return st.enter_context(nc.sbuf_tensor(name, shape, dt))

        def sem(name):
            return st.enter_context(nc.semaphore(name))

        w1 = sb("w1", [128, 2, F])
        w2 = sb("w2", [128, 2, FC, D])
        b1 = sb("b1", [128, 2, FC])
        b2 = sb("b2", [1, 2, D])
        cur = sb("cur", [128, 2, SL], i32)
        x = sb("x_rows", [128, 2, SL, GW])
        xT = sb("xT", [128, 2, 512])
        hid = sb("hid_e", [128, 2, FC, 512])
        y = sb("y_rows", [128, 2, SL, D])
        ps = st.enter_context(nc.psum_tensor("ffn_ps", [128, 8, 512], f32))
        w_in = [sem("w_in0"), sem("w_in1")]
        gathered = [sem("gathered0"), sem("gathered1")]
        cur_ready, xT_ps, xT_ready, up_ps, hid_ready, down_ps, y_ready, added = (sem(n) for n in (
            "cur_ready", "e_xT_ps", "e_xT_ready", "e_up_ps", "e_hid_ready", "e_down_ps", "e_y_ready", "added"))
        block = st.enter_context(nc.Block())

        W_IN = 16 * (3 + FC)

        def experts(engine, body):
            body(0)
            with engine.Fori(0, EXPERTS // 2 - 1) as q:
                body(q + 1)

        def later(q):
            return type(q) is not int

        @block.sync
        def _(sp):
            def body(q):
                for u in range(2):
                    e = q * 2 + u
                    if later(q):
                        sp.wait_ge(down_ps, q * 4 + (2 * u - 2))
                    sp.dma_start(w1[:, u, :], A["W1"][e]).then_inc(w_in[u], 16)
                    sp.dma_start(w2[:, u, :, :], A["W2"][e].rearrange("(c p) d -> p c d", p=128)).then_inc(w_in[u], 16)
                    for f in range(FC):
                        sp.dma_start(b1[:, u, f:f + 1], A["b1"][e, f * 128:(f + 1) * 128].rearrange("(p a) -> p a", a=1)).then_inc(w_in[u], 16)
                    sp.dma_start(b2[:, u, :], A["b2"][e].rearrange("(a d) -> a d", a=1)).then_inc(w_in[u], 16)
            experts(sp, body)

        @block.gpsimd
        def _(pool):
            def gather(e, u):
                if type(e) is not int or e >= 2:
                    pool.wait_ge(added, e * (SL * 16) - SL * 16)
                    pool.wait_ge(y_ready, e * 2 - 2)
                pool.sem_inc(passed, 1)
                pool.tensor_copy(cur[:, u, :], index_all[:, bass.ds(e, 1), :].rearrange("p a s -> p (a s)")).then_inc(cur_ready, 1)
                pool.wait_ge(cur_ready, e + 1)
                pool.sem_inc(passed, 1)
                for i in range(SL):
                    pool.indirect_dma_start(out=x[:, u, i, :], out_offset=None, in_=table_rows,
                                            in_offset=bass.IndirectOffsetOnAxis(ap=cur[:, u, i:i + 1], axis=0)).then_inc(gathered[u], 16)

            def scatter(e, u):
                if type(e) is not int or e >= 1:
                    pool.wait_ge(added, e * (SL * 16))
                pool.wait_ge(y_ready, e * 2 + 2)
                pool.sem_inc(passed, 1)
                for i in range(SL):
                    pool.indirect_dma_start(out=out_rows, out_offset=bass.IndirectOffsetOnAxis(ap=cur[:, u, i:i + 1], axis=0),
                                            in_=y[:, u, i, :], in_offset=None, compute_op=ALU.add).then_inc(added, 16)
            gather(0, 0)
            gather(1, 1)
            scatter(0, 0)
            with pool.Fori(0, EXPERTS // 2 - 1) as q:
                for u in range(2):
                    gather(q * 2 + (2 + u), u)
                    scatter(q * 2 + (1 + u), 1 - u)
            scatter(EXPERTS - 1, 1)
            pool.wait_ge(added, EXPERTS * SL * 16)

        @block.scalar
        def _(act):
            def turned(n, c):
                act.wait_ge(xT_ps, n + 1)
                if type(n) is not int or n >= 2:
                    act.wait_ge(up_ps, n * FC - FC)
                act.activation(xT[:, c, :], ps[:, 7 * c, :], ACT.Copy).then_inc(xT_ready, 1)

            def gelu(n, c, u, q):
                if c == 0:
                    act.wait_ge(w_in[u], q * W_IN + W_IN)
                if type(n) is not int or n >= 2:
                    act.wait_ge(down_ps, n - 1)
                for f in range(FC):
                    act.wait_ge(up_ps, n * FC + (f + 1))
                    act.activation(hid[:, c, f, :], ps[:, 1 + f, :], ACT.Gelu, bias=b1[:, u, f:f + 1]).then_inc(hid_ready, 1)

            def body(q):
                for u in range(2):
                    for c in range(2):
                        n = q * 4 + (2 * u + c)
                        turned(n, c)
                        gelu(n, c, u, q)
            experts(act, body)

        @block.tensor
        def _(pe):
            def up(q, u, c):
                n = q * 4 + (2 * u + c)
                if c == 0:
                    pe.wait_ge(gathered[u], q * (SL * 16) + SL * 16)
                if type(n) is not int or n >= 2:
                    pe.wait_ge(xT_ready, n - 1)
                for s in range(4):
                    last = pe.transpose(ps[:, 7 * c, s * 128:(s + 1) * 128], x[:, u, 4 * c + s, 0:D], ident[:, :])
                last.then_inc(xT_ps, 1)
                if c == 0:
                    pe.wait_ge(w_in[u], q * W_IN + W_IN)
                pe.wait_ge(xT_ready, n + 1)
                for f in range(FC):
                    if type(n) is not int or n >= 1:
                        pe.wait_ge(hid_ready, n * FC + (f + 1 - FC))
                    pe.matmul(ps[:, 1 + f, :], w1[:, u, f * 128:(f + 1) * 128], xT[:, c, :], start=True, stop=True).then_inc(up_ps, 1)

            def down(q, u, c):
                n = q * 4 + (2 * u + c)
                pe.wait_ge(hid_ready, n * FC + FC)
                if type(n) is not int or n >= 2:
                    pe.wait_ge(y_ready, n - 1)
                for s in range(4):
                    dst = ps[:, 5 + c, s * D:(s + 1) * D]
                    pe.matmul(dst, ones[0:1, :], b2[0:1, u, :], start=True, stop=False)
                    for f in range(FC):
                        last = pe.matmul(dst, hid[:, c, f, s * 128:(s + 1) * 128], w2[:, u, f, :], start=False, stop=(f == FC - 1))
                last.then_inc(down_ps, 1)

            def body(q):
                for u in range(2):
                    for c in range(2):
                        up(q, u, c)
                        down(q, u, c)
            experts(pe, body)

        @block.vector
        def _(dve):
            def body(q):
                for u in range(2):
                    if later(q):
                        dve.wait_ge(added, q * (2 * SL * 16) + (u - 1) * (SL * 16))
                    dve.wait_ge(gathered[u], q * (SL * 16) + SL * 16)
                    for c in range(2):
                        dve.wait_ge(down_ps, q * 4 + (2 * u + c + 1))
                        for s in range(4):
                            last = dve.tensor_scalar(y[:, u, 4 * c + s, :], ps[:, 5 + c, s * D:(s + 1) * D],
                                                     x[:, u, 4 * c + s, bass.ds(q * 2 + (D + u), 1)], None, ALU.mult)
                        last.then_inc(y_ready, 1)
            experts(dve, body)


def kernel(**inputs):
    import numpy as _np
    import concourse.bacc as _bacc
    from concourse import mybir as _mybir
    from concourse.bass_utils import run_bass_kernel_spmd as _run

    x = _np.asarray(inputs["x"])
    B, C, IMG, _ = x.shape
    P = 16
    G = IMG // P
    D = inputs["L0_tok_conv_w"].shape[1]
    arrays = {"x": _np.ascontiguousarray(x.reshape(B, C, G, P, G, P).transpose(1, 3, 5, 0, 2, 4)).reshape(-1, 128, B * G * G)}
    for name, a in inputs.items():
        if name != "x":
            arrays[name.replace("L0_tok_", "").replace("L0_ffn_", "")] = _np.ascontiguousarray(a)
    nc = _bacc.Bacc("TRN2", target_bir_lowering=False, num_devices=1)
    A = {n: nc.dram_tensor(f"in_{n}", a.shape, _mybir.dt.from_np(a.dtype), kind="ExternalInput").ap() for n, a in arrays.items()}
    out = nc.dram_tensor("out_dram", (B, G * G + 1, D), _mybir.dt.float32, kind="ExternalOutput").ap()
    build(nc, A, out)
    r = _run(nc, [{f"in_{n}": a for n, a in arrays.items()}], core_ids=[0])
    return r.results[0]["out_dram"]
```

```python
def build(nc, A, out):
    import concourse.bass as bass
    from concourse import mybir
    from contextlib import ExitStack

    f32, bf16, i32 = mybir.dt.float32, mybir.dt.bfloat16, mybir.dt.int32
    ALU = mybir.AluOpType
    ACT = mybir.ActivationFunctionType
    AX = mybir.AxisListType

    IMAGES, NTOK, D = out.shape
    DEPTH = A["ln1_w"].shape[0]
    HID = A["fc1_w"].shape[2]
    HEADS = 8
    HD = D // HEADS
    R = (NTOK + 1) // 2
    P1 = R - 1
    W = 2 * R
    W2 = 2 * W
    PAIRS = IMAGES // 2
    TILES = 2 * IMAGES
    CH = A["x"].shape[0]
    EPS = 1e-5
    SCALE = float(HD) ** -0.5
    NP = 8
    NB = 4
    NZ = 4

    top = ExitStack()
    with top:
        def scope_tools(stack):
            def sb(name, shape, dt=f32):
                return stack.enter_context(nc.sbuf_tensor(name, shape, dt))

            def pb(name, shape, dt=f32):
                return stack.enter_context(nc.psum_tensor(name, shape, dt))

            def sem(name):
                return stack.enter_context(nc.semaphore(name))
            return sb, pb, sem

        sb, pb, sem = scope_tools(top)
        h = sb("h", [R, TILES, D])
        ident = sb("ident", [128, 128])
        ones = sb("ones", [128, 128])
        passed = sem("passed")
        with ExitStack() as st:
            sb, pb, sem = scope_tools(st)
            NX = 3
            xt = sb("xt", [128, NX, CH, 4 * P1])
            wconv = sb("wconv", [128, CH, D])
            pos = sb("pos", [P1, 2, D])
            convb = sb("convb", [P1, D])
            posb = sb("posb", [P1, 2, D])
            cls = sb("cls", [1, 2, D])
            clsrow = sb("clsrow", [1, D])
            acc = pb("acc", [128, 2, 4, D])

            x_in = [sem(f"x_in{i}") for i in range(NX)]
            w_in, consts_in, tok_ready, tok_taken = sem("w_in"), sem("consts_in"), sem("tok_ready"), sem("tok_taken")
            posb_ready, cls_ready, cls_out, ident_zero = sem("posb_ready"), sem("cls_ready"), sem("cls_out"), sem("ident_zero")

            block = st.enter_context(nc.Block())

            @block.sync
            def _(sp):
                sp.dma_start(wconv[:, :, :], A["conv_w"].rearrange("(c p) d -> p c d", p=128)).then_inc(w_in, 16)

                def load(pair, slot):
                    sp.dma_start(xt[:, slot, :, :], A["x"][:, :, bass.ds(pair * (4 * P1), 4 * P1)]
                                 .rearrange("c p n -> p c n")).then_inc(x_in[slot], 16)

                for i in range(NX):
                    load(i, i)
                with sp.Fori(0, PAIRS // NX - 1) as q:
                    for u in range(NX):
                        sp.wait_ge(tok_ready, q * NX + (u + 1))
                        load(q * NX + (NX + u), u)
                for i in range(PAIRS // NX * NX, PAIRS):
                    sp.wait_ge(tok_ready, i - NX + 1)
                    load(i, i % NX)
                sp.wait_ge(cls_ready, 1)
                sp.dma_start(h[P1:R, :, :], clsrow[0:1, :].rearrange("p (a d) -> p a d", a=1)
                             .to_broadcast([1, TILES, D])).then_inc(cls_out, 16)
                sp.wait_ge(cls_out, 16)

            @block.scalar
            def _(act):
                act.dma_start(pos[:, :, :], A["pos_embed"][0, 1:NTOK, :].rearrange("(t p) d -> p t d", p=P1)).then_inc(consts_in, 16)
                act.dma_start(convb[:, :], A["conv_b"].partition_broadcast(P1)).then_inc(consts_in, 16)
                act.dma_start(cls[:, 0, :], A["cls_token"][0]).then_inc(consts_in, 16)
                act.dma_start(cls[:, 1, :], A["pos_embed"][0, 0:1, :]).then_inc(consts_in, 16)

            @block.gpsimd
            def _(pool):
                pool.memset(ones[:, :], 1.0)
                pool.memset(ident[:, :], 0.0).then_inc(ident_zero, 1)
                pool.wait_ge(ident_zero, 1)
                pool.affine_select(out=ident[:, :], in_=ident[:, :], compare_op=ALU.not_equal, fill=1.0,
                                   base=0, pattern=[[-1, 128]], channel_multiplier=1)

            @block.tensor
            def _(pe):
                pe.wait_ge(w_in, 16)

                def embed(slot, b):
                    for t in range(4):
                        for c in range(CH):
                            last = pe.matmul(acc[0:P1, b, t, :], xt[:, slot, c, t * P1:(t + 1) * P1], wconv[:, c, :],
                                             start=(c == 0), stop=(c == CH - 1))
                    last.then_inc(tok_ready, 1)

                for i in range(2):
                    pe.wait_ge(x_in[i], 16)
                    embed(i, i)
                with pe.Fori(0, (PAIRS - 2) // 6) as q:
                    for u in range(6):
                        slot = (u + 2) % NX
                        pe.wait_ge(x_in[slot], q * 32 + 16 * ((u + 2) // NX + 1))
                        pe.wait_ge(tok_taken, q * 6 + (u + 1))
                        embed(slot, u % 2)

            @block.vector
            def _(dve):
                dve.wait_ge(consts_in, 64)
                for t in range(2):
                    last = dve.tensor_tensor(posb[:, t, :], pos[:, t, :], convb[:, :], ALU.add)
                last.then_inc(posb_ready, 1)
                dve.tensor_tensor(clsrow[:, :], cls[:, 0, :], cls[:, 1, :], ALU.add).then_inc(cls_ready, 1)
                dve.wait_ge(posb_ready, 1)
                with dve.Fori(0, PAIRS // 2) as q:
                    for b in range(2):
                        dve.wait_ge(tok_ready, q * 2 + (b + 1))
                        dve.wait_ge(posb_ready, 1)
                        for im in range(2):
                            last = dve.tensor_tensor(h[0:P1, bass.ds(q * 8 + (4 * b + 2 * im), 2), :],
                                                     acc[0:P1, b, 2 * im:2 * im + 2, :], posb[:, :, :], ALU.add)
                        last.then_inc(tok_taken, 1)
        with ExitStack() as st:
            sb, pb, sem = scope_tools(st)
            wqkv_raw = sb("wqkv_raw", [128, 3 * D])
            wproj_raw = sb("wproj_raw", [128, D])
            wfc1_raw = sb("wfc1_raw", [128, HID])
            wfc2_raw = sb("wfc2_raw", [128, 2, D])
            cols = sb("cols", [128, 4])
            qkvb = sb("qkvb", [128, 3])
            fc1b = sb("fc1b", [128, 2])
            rows = sb("rows", [1, 2, D])
            wqkv = sb("wqkv", [128, 3 * D])
            wproj = sb("wproj", [128, D])
            wfc1 = sb("wfc1", [128, HID])
            wfc2 = sb("wfc2", [128, 2, D])
            bqkv = sb("bqkv", [128, 3])
            bfc1 = sb("bfc1", [128, 2])
            bv_wide = sb("bv_wide", [128, R])
            bproj = sb("bproj", [R, D])
            bfc2 = sb("bfc2", [R, D])

            eps_t = sb("eps_t", [R, 4])
            mhalf = sb("mhalf", [R, 4])
            stats = sb("stats", [R, 4, 6])
            mv = sb("mv", [R, 4, 2])
            rstd = sb("rstd", [R, 4])
            xc = sb("xc", [R, 4, D])
            y = sb("y", [R, 4, D])
            yT = sb("yT", [128, W2])
            parts = sb("parts", [128, 2, 3, W2], bf16)
            rest = sb("rest", [128, 2, W2])
            Q = sb("Q", [98, NB, HEADS, W2], bf16)
            K = sb("K", [98, NB, HEADS, W2], bf16)
            V = sb("V", [R, NB, 4, HEADS, 32])
            negmax = sb("negmax", [R, 2, 2, HEADS])
            mhi = sb("mhi", [2 * HEADS, 2, R], bf16)
            mlo = sb("mlo", [2 * HEADS, 2, R], bf16)
            probs = sb("probs", [R, NP, 2 * W])
            rsum = sb("rsum", [R, 2 * HEADS])
            oU = sb("oU", [128, 2 * W])
            o = sb("o", [R, 2, D])
            oT = sb("oT", [128, W])
            mv2 = sb("mv2", [R, NZ, 4, 2])
            var2 = sb("var2", [R, 4])
            rstd2 = sb("rstd2", [R, NZ, 4])
            z = sb("z", [R, NZ, 4, D])
            zT = sb("zT", [128, 2, W2])
            hid = sb("hid", [128, 2, 2, W2])
            q_scratch = nc.dram_tensor("q_scratch", [HEADS, 3, HD, W2], bf16, kind="Internal").ap()
            k_scratch = nc.dram_tensor("k_scratch", [3, HEADS, HD, W2], bf16, kind="Internal").ap()

            ps = pb("ps", [128, 8, 512])

            raw_in, folded, prep_mm = sem("raw_in"), sem("folded"), sem("prep_mm")
            bias_ready, bvw_ready, consts = sem("bias_ready"), sem("bvw_ready"), sem("consts")
            weights_ready = sem("weights_ready")
            ln_stats, ln_aggr, ln_var, ln_rstd, ln_centred, y_ready = (sem(n) for n in (
                "ln_stats", "ln_aggr", "ln_var", "ln_rstd", "ln_centred", "y_ready"))
            hbias = sem("hbias")
            yT_ps, yT_ready = sem("yT_ps"), sem("yT_ready")
            qk_ps, part1, rest_ready, part2, parts_ready = (sem(n) for n in (
                "qk_ps", "part1", "rest_ready", "part2", "parts_ready"))
            qk_saved, qk_loaded = [sem("q_saved"), sem("k_saved")], sem("qk_loaded")
            v_ps, v_ready = sem("v_ps"), sem("v_ready")
            mx_ps, mx_done = sem("mx_ps"), sem("mx_done")
            mT_ps, mhi_ready, mlo_ready = sem("mT_ps"), sem("mhi_ready"), sem("mlo_ready")
            max_loaded = [sem("max_loaded0"), sem("max_loaded1")]
            st_ps, probs_ready, probs_used = sem("st_ps"), sem("probs_ready"), sem("probs_used")
            oU_ready, oU_turned, rsum_ready, o_ready = sem("oU_ready"), sem("oU_turned"), sem("rsum_ready"), sem("o_ready")
            oT_ps, oT_ready, proj_ps, attn_done = (sem(n) for n in ("oT_ps", "oT_ready", "proj_ps", "attn_done"))
            ln2_stats, ln2_aggr, ln2_var, ln2_rstd, z_ready, hbias2 = (sem(n) for n in (
                "ln2_stats", "ln2_aggr", "ln2_var", "ln2_rstd", "z_ready", "hbias2"))
            zT_ps, zT_ready, hid_ps, hid_ready, fc2_ps, mlp_done = (sem(n) for n in (
                "zT_ps", "zT_ready", "hid_ps", "hid_ready", "fc2_ps", "mlp_done"))

            block = st.enter_context(nc.Block())

            def slots(engine, layer, body):
                def on(k):
                    return {n for n, lag in (("stats", 5), ("norm", 4), ("project", 3), ("maxima", 1), ("now", 0), ("tail", -1))
                            if 0 <= k + lag < PAIRS}
                for k in range(-5, 1):
                    body(k, k % NB, on(k))
                with engine.Fori(0, (PAIRS - 6) // NB) as q:
                    for u in range(NB):
                        body(q * NB + (u + 1), (u + 1) % NB, on(1))
                for k in range(1 + (PAIRS - 6) // NB * NB, PAIRS + 1):
                    body(k, k % NB, on(k))


            def bank_T(b, s):
                bank = (2 * HEADS * b + s) % 3
                before = [(2 * HEADS * ((b - 1) % NB if e < 0 else b) + e % (2 * HEADS)) % 3 for e in range(s - 1, s - 5, -1)]
                return bank, before.index(bank) + 1

            MISC = [("mT1", "now"), ("yT", "project"), ("q", "project"), ("k", "project"), ("mT0", "maxima"),
                    ("oT1", "tail"), ("v", "project"), ("oT0", "now")]
            LEAD = {"project": 3, "maxima": 1, "now": 0, "tail": -1}

            @block.sync
            def _(sp):
                with sp.Fori(0, DEPTH) as l:
                    sp.wait_ge(weights_ready, l)
                    sp.dma_start(wqkv_raw[:, :], A["qkv_w"][l]).then_inc(raw_in, 16)
                    sp.dma_start(wproj_raw[:, :], A["proj_w"][l]).then_inc(raw_in, 16)
                    sp.dma_start(wfc1_raw[:, :], A["fc1_w"][l]).then_inc(raw_in, 16)
                    sp.dma_start(wfc2_raw[:, :, :], A["fc2_w"][l].rearrange("(c p) d -> p c d", p=128)).then_inc(raw_in, 16)
                    for i, n in enumerate(("ln1_w", "ln1_b", "ln2_w", "ln2_b")):
                        sp.dma_start(cols[:, i:i + 1], A[n][l].rearrange("(p a) -> p a", a=1)).then_inc(raw_in, 16)
                    for i in range(3):
                        sp.dma_start(qkvb[:, i:i + 1], A["qkv_b"][l, i * D:(i + 1) * D].rearrange("(p a) -> p a", a=1)).then_inc(raw_in, 16)
                    for i in range(2):
                        sp.dma_start(fc1b[:, i:i + 1], A["fc1_b"][l, i * D:(i + 1) * D].rearrange("(p a) -> p a", a=1)).then_inc(raw_in, 16)
                    sp.dma_start(rows[:, 0, :], A["proj_b"][l].rearrange("(a p) -> a p", a=1)).then_inc(raw_in, 16)
                    sp.dma_start(rows[:, 1, :], A["fc2_b"][l].rearrange("(a p) -> a p", a=1)).then_inc(raw_in, 16)

                    def load_max(b, im, n):
                        sp.wait_ge(mlo_ready, n)
                        for i, m in enumerate((mhi, mlo)):
                            for t in range(2):
                                sp.dma_start(Q[96 + i:97 + i, b, :, im * W + t * R:im * W + (t + 1) * R],
                                             m[t * HEADS:(t + 1) * HEADS, im, :]).then_inc(max_loaded[im], 16)

                    def body(k, b, on):
                        it = l * PAIRS + k
                        b1, b3 = (b + 1) % NB, (b + 3) % NB
                        if "now" in on:
                            load_max(b, 1, it * 2 + 2)
                        if "project" in on:
                            n = it + 3
                            sp.wait_ge(qk_loaded, n * 144)
                            sp.wait_ge(parts_ready, n * 2 + 1)
                            for j in range(3):
                                sp.dma_start(q_scratch[:, j, :, :], parts[:, 0, j, :]).then_inc(qk_saved[0], 16)
                        if "maxima" in on:
                            load_max(b1, 0, it * 2 + 3)
                        if "project" in on:
                            sp.wait_ge(parts_ready, n * 2 + 2)
                            sp.dma_start(k_scratch.rearrange("j h d t -> (h d) j t"), parts[:, 1, :, :]).then_inc(qk_saved[1], 16)
                            if "tail" in on:
                                sp.wait_ge(st_ps, it * 2 * HEADS)
                            sp.wait_ge(qk_saved[0], n * 48 + 48)
                            for r0, j0, m in ((0, 0, 3), (48, 0, 2), (80, 0, 1)):
                                sp.dma_start(Q[r0:r0 + m * HD, b3, :, :], q_scratch[:, j0:j0 + m].rearrange("h j d t -> (j d) h t")).then_inc(qk_loaded, 16)
                            sp.wait_ge(qk_saved[1], n * 16 + 16)
                            for r, j in enumerate((0, 0, 0, 1, 1, 2)):
                                sp.dma_start(K[r * HD:(r + 1) * HD, b3, :, :], k_scratch[j].rearrange("h d t -> d h t")).then_inc(qk_loaded, 16)
                    slots(sp, l, body)

            @block.gpsimd
            def _(pool):
                pool.memset(eps_t[:, :], EPS)
                pool.memset(mhalf[:, :], -0.5)
                pool.memset(V[:, :, :, :, :], 1.0).then_inc(consts, 1)
                pool.wait_ge(consts, 1)
                pool.memset(K[96:98, :, :, :], 1.0).then_inc(consts, 1)
                pool.wait_ge(consts, 2)

                def normalise(pair, n, s_aggr, s_var, s_rstd, s_centred, s_out, s_bias, dst, dst_free, bias_row):
                    pool.wait_ge(s_out, n - 1)
                    pool.wait_ge(s_aggr, n)
                    pool.tensor_tensor(rstd[:, :], mv[:, :, 1], eps_t[:, :], ALU.add).then_inc(s_var, 1)
                    pool.wait_ge(s_var, n)
                    pool.tensor_tensor(rstd[:, :], rstd[:, :], mhalf[:, :], ALU.pow).then_inc(s_rstd, 1)
                    pool.wait_ge(s_rstd, n)
                    pool.sem_inc(passed, 1)
                    hp = h[:, bass.ds(pair * 4, 4), :]
                    pool.tensor_tensor(xc[:, :, :], hp, mv[:, :, 0:1].to_broadcast([R, 4, D]), ALU.subtract).then_inc(s_centred, 1)
                    dst_free()
                    pool.wait_ge(s_centred, n)
                    pool.tensor_tensor(dst, xc[:, :, :], rstd[:, :].rearrange("p (t a) -> p t a", a=1).to_broadcast([R, 4, D]), ALU.mult).then_inc(s_out, 1)
                    pool.tensor_tensor(hp, hp, bias_row[:, :].rearrange("p (a d) -> p a d", a=1).to_broadcast([R, 4, D]), ALU.add).then_inc(s_bias, 1)

                with pool.Fori(0, DEPTH) as l:
                    pool.wait_ge(weights_ready, l + 1)

                    def body(k, b, on):
                        it = l * PAIRS + k
                        if "norm" in on:
                            n = it + 4

                            def y_free():
                                pool.wait_ge(yT_ps, n)
                            normalise(k + 4, n + 1, ln_aggr, ln_var, ln_rstd, ln_centred, y_ready, hbias, y[:, :, :], y_free, bproj)
                        if "project" in on:
                            for i in range(2):
                                n = it * 2 + (6 + i)
                                pool.wait_ge(part2, n + 1)
                                pool.tensor_tensor(parts[:, i, 2, :], rest[:, i, :], parts[:, i, 1, :], ALU.subtract).then_inc(parts_ready, 1)
                    slots(pool, l, body)

                    def factor(p, b):
                        n = l * PAIRS + p
                        pool.wait_ge(ln2_rstd, n)
                        pool.wait_ge(ln2_aggr, n + 1)
                        pool.tensor_tensor(var2[:, :], mv2[:, b, :, 1], eps_t[:, :], ALU.add).then_inc(ln2_var, 1)
                        if type(p) is not int or p >= NZ:
                            pool.wait_ge(z_ready, n - (NZ - 1))
                        pool.wait_ge(ln2_var, n + 1)
                        pool.tensor_tensor(rstd2[:, b, :], var2[:, :], mhalf[:, :], ALU.pow).then_inc(ln2_rstd, 1)

                    def bias(p):
                        n = l * PAIRS + p
                        pool.wait_ge(z_ready, n + 1)
                        pool.sem_inc(passed, 1)
                        hp = h[:, bass.ds(p * 4, 4), :]
                        pool.tensor_tensor(hp, hp, bfc2[:, :].rearrange("p (a d) -> p a d", a=1).to_broadcast([R, 4, D]), ALU.add).then_inc(hbias2, 1)
                    factor(0, 0)
                    factor(1, 1)

                    def both(p, u):
                        factor(p, u % NZ)
                        bias(p - 2)
                    for p in range(2, NZ):
                        both(p, p)
                    with pool.Fori(0, PAIRS // NZ - 1) as q:
                        for u in range(NZ):
                            both(q * NZ + (NZ + u), u)
                    for p in range(PAIRS - 2, PAIRS):
                        bias(p)


            RAW = 15 * 16

            @block.scalar
            def _(act):
                act.wait_ge(consts, 2)
                with act.Fori(0, DEPTH) as l:
                    act.wait_ge(weights_ready, l + 1)

                    def body(k, b, on):
                        it = l * PAIRS + k
                        b3 = (b + 3) % NB

                        def exps(g):
                            if "now" not in on:
                                return
                            n = it * (2 * HEADS)
                            if g % 4 == 0 and (type(k) is not int or k > 0 or g >= NP):
                                act.wait_ge(probs_used, it * 4 + (g // 4 - 1))
                            act.wait_ge(st_ps, n + (g + 1))
                            act.activation(probs[:, g % NP, :], ps[0:R, bank_T(b, g)[0], 0:2 * W], ACT.Exp, scale=SCALE).then_inc(probs_ready, 1)

                        def max_high(im, pair, stage):
                            if stage in on:
                                n = pair * 2 + im
                                act.wait_ge(mT_ps, n + 1)
                                act.wait_ge(max_loaded[im], pair * 64)
                                act.activation(mhi[:, im, :], ps[0:2 * HEADS, 7, 0:R], ACT.Copy).then_inc(mhi_ready, 1)

                        def part_one(i):
                            if "project" in on:
                                n = it + 3
                                act.wait_ge(qk_ps, n * 2 + (i + 1))
                                act.wait_ge(qk_saved[i], n * (48, 16)[i])
                                act.activation(parts[:, i, 0, :], ps[:, 7, 0:W2], ACT.Identity, bias=bqkv[:, i:i + 1]).then_inc(part1, 1)

                        def part_two(i):
                            if "project" in on:
                                act.wait_ge(rest_ready, it * 2 + (6 + i + 1))
                                act.activation(parts[:, i, 1, :], rest[:, i, :], ACT.Copy).then_inc(part2, 1)

                        def output(im, pair, stage):
                            if stage in on:
                                n = pair * 2 + im
                                act.wait_ge(oU_turned, n)
                                act.wait_ge(probs_used, pair * 4 + (2 * im + 2))
                                act.activation(oU[:, :], ps[:, 6, 0:2 * W], ACT.Copy).then_inc(oU_ready, 1)

                        def out_T(im, pair, stage):
                            if stage in on:
                                n = pair * 2 + im
                                act.wait_ge(oT_ps, n + 1)
                                act.wait_ge(proj_ps, n)
                                act.activation(oT[:, :], ps[:, 7, 0:W], ACT.Copy).then_inc(oT_ready, 1)

                        for s in range(2 * HEADS):
                            if s == 1:
                                out_T(0, it - 1, "tail")
                            if s == 2:
                                max_high(1, it, "now")
                            if s == 3 and "project" in on:
                                act.wait_ge(yT_ps, it + 4)
                                act.wait_ge(v_ps, it + 3)
                                act.activation(yT[:, :], ps[:, 7, 0:W2], ACT.Copy).then_inc(yT_ready, 1)
                            if s == 4:
                                output(1, it - 1, "tail")
                            if s == 5:
                                part_one(0)
                            if s == 6:
                                part_two(0)
                            if s == 7:
                                part_one(1)
                            if s == 9:
                                part_two(1)
                            if s == 10:
                                max_high(0, it + 1, "maxima")
                            if s == 11:
                                out_T(1, it - 1, "tail")
                            if s == 12:
                                output(0, it, "now")
                            if s == 14 and "project" in on:
                                act.wait_ge(v_ps, it + 4)
                                if "tail" in on:
                                    act.wait_ge(probs_used, it * 4)
                                act.activation(V[:, b3, :, :, 0:HD], ps[0:R, 7, :].rearrange("p (t h d) -> p t h d", t=4, h=HEADS),
                                               ACT.Copy).then_inc(v_ready, 1)
                            exps(s)
                    slots(act, l, body)

                    def transposed(p, b):
                        n = l * PAIRS + p
                        act.wait_ge(zT_ps, n + 1)
                        if type(p) is not int or p >= 2:
                            act.wait_ge(hid_ps, n - 1)
                        act.activation(zT[:, b, :], ps[:, b, 0:W2], ACT.Copy).then_inc(zT_ready, 1)

                    def gelu(p, b):
                        n = l * PAIRS + p
                        act.wait_ge(hid_ps, n + 1)
                        if type(p) is not int or p >= 2:
                            act.wait_ge(fc2_ps, n - 1)
                        for c in range(2):
                            last = act.activation(hid[:, b, c, :], ps[:, 2 + 2 * b + c, 0:W2], ACT.Gelu, bias=bfc1[:, c:c + 1])
                        last.then_inc(hid_ready, 1)

                    transposed(0, 0)
                    transposed(1, 1)
                    gelu(0, 0)
                    with act.Fori(0, (PAIRS - 2) // 2) as q:
                        for u in range(2):
                            transposed(q * 2 + (2 + u), u)
                            gelu(q * 2 + (1 + u), 1 - u)
                    gelu(PAIRS - 1, 1)

            @block.tensor
            def _(pe):
                with pe.Fori(0, DEPTH) as l:
                    pe.wait_ge(raw_in, (l + 1) * RAW)
                    pe.wait_ge(mlp_done, l * PAIRS)
                    for i in range(3):
                        pe.matmul(ps[:, 0, i:i + 1], wqkv_raw[:, i * D:(i + 1) * D], cols[:, 1:2], start=True, stop=True)
                    for i in range(2):
                        last = pe.matmul(ps[:, 0, 3 + i:4 + i], wfc1_raw[:, i * D:(i + 1) * D], cols[:, 3:4], start=True, stop=True)
                    last.then_inc(prep_mm, 1)
                    pe.wait_ge(bvw_ready, l + 1)
                    pe.matmul(ps[0:R, 1, 0:D], bv_wide[:, :], wproj_raw[:, :], start=True, stop=False)
                    pe.matmul(ps[0:R, 1, 0:D], ones[0:1, 0:R], rows[:, 0, :], start=False, stop=True)
                    pe.matmul(ps[0:R, 2, 0:D], ones[0:1, 0:R], rows[:, 1, :], start=True, stop=True).then_inc(prep_mm, 1)
                    pe.wait_ge(weights_ready, l + 1)

                    def body(k, b, on):
                        it = l * PAIRS + k
                        b1, b3 = (b + 1) % NB, (b + 3) % NB

                        def freed(use, pair):
                            kind, im = use.rstrip("01"), int(use[-1]) if use[-1] in "01" else 0
                            s, per, at = {"yT": (yT_ready, 1, 0), "v": (v_ready, 1, 0), "mT": (mlo_ready, 2, im),
                                          "q": (rest_ready, 2, 0), "k": (rest_ready, 2, 1), "oT": (oT_ready, 2, im)}[kind]
                            pe.wait_ge(s, pair * per + (at + 1))

                        def bank(use):
                            names = [u for u, _ in MISC]
                            i = names.index(use)
                            if MISC[i][1] not in on:
                                return False
                            before = [u for u in MISC[:i] if u[1] in on]
                            if before:
                                freed(before[-1][0], it + LEAD[before[-1][1]])
                            elif type(k) is not int or k >= 1:
                                freed("oT0", it - 1)
                            elif k >= -2:
                                freed("v", it + 2)
                            return True

                        def scores_T(s):
                            im, hd = s // HEADS, s % HEADS
                            bank, before = bank_T(b, s)
                            if type(k) is not int or k > 0 or s >= before:
                                pe.wait_ge(probs_ready, it * (2 * HEADS) + (s - before + 1))
                            if hd == 0:
                                pe.wait_ge(max_loaded[im], it * 64 + 64)
                            for t in range(2):
                                last = pe.matmul(ps[0:R, bank, t * W:(t + 1) * W], K[0:98, b, hd, im * W + t * R:im * W + (t + 1) * R],
                                                 Q[0:98, b, hd, im * W:(im + 1) * W], start=True, stop=True)
                            last.then_inc(st_ps, 1)

                        def scores(s):
                            im, hd = s // HEADS, s % HEADS
                            if s == 0:
                                pe.wait_ge(qk_loaded, it * 144 + 288)
                            if type(k) is not int or k > -1 or s >= 2:
                                pe.wait_ge(mx_done, it * 16 + (16 + s - 1))
                            for t in range(2):
                                last = pe.matmul(ps[0:R, 4 + s % 2, t * W:(t + 1) * W], Q[0:96, b1, hd, im * W + t * R:im * W + (t + 1) * R],
                                                 K[0:96, b1, hd, im * W:(im + 1) * W], start=True, stop=True)
                            last.then_inc(mx_ps, 1)

                        def values(g, pair, bv):
                            im, c = g // 2, g % 2
                            if g == 0:
                                pe.wait_ge(v_ready, pair + 1)
                            if c == 0:
                                pe.wait_ge(oU_ready, pair * 2 + im)
                            pe.wait_ge(probs_ready, pair * (2 * HEADS) + 4 * (g + 1))
                            for tk, rows_k in ((0, R), (1, P1)):
                                for i in range(4):
                                    hd = 4 * c + i
                                    last = pe.matmul(ps[32 * i:32 * i + 32, 6, c * W:(c + 1) * W], V[0:rows_k, bv, im * 2 + tk, hd, :],
                                                     probs[0:rows_k, (4 * g + i) % NP, tk * W:(tk + 1) * W], start=(tk == 0), stop=(tk == 1))
                            last.then_inc(probs_used, 1)

                        def turn(im, pair):
                            pe.wait_ge(oU_ready, pair * 2 + (im + 1))
                            if im == 1 or "tail" in on:
                                pe.wait_ge(attn_done, pair * 2 + im)
                            for t in range(2):
                                for c in range(2):
                                    last = pe.transpose(ps[0:R, 3, (2 * t + c) * 128:(2 * t + c + 1) * 128], oU[:, c * W + t * R:c * W + (t + 1) * R], ident[:, :])
                            last.then_inc(oU_turned, 1)

                        def max_T(im, pair):
                            pe.wait_ge(mx_done, pair * 16 + (im + 1) * HEADS)
                            pe.transpose(ps[0:2 * HEADS, 7, 0:R], negmax[:, im, :, :].rearrange("p t h -> p (t h)"), ident[0:R, 0:R]).then_inc(mT_ps, 1)

                        def out_T(im, pair):
                            pe.wait_ge(o_ready, pair * 2 + (im + 1))
                            for t in range(2):
                                last = pe.transpose(ps[:, 7, t * R:(t + 1) * R], o[:, t, :], ident[0:R, 0:R])
                            last.then_inc(oT_ps, 1)

                        def proj(im, pair):
                            pe.wait_ge(oT_ready, pair * 2 + (im + 1))
                            for t in range(2):
                                last = pe.matmul(ps[0:R, 3, t * D:(t + 1) * D], oT[:, t * R:(t + 1) * R], wproj[:, :], start=True, stop=True)
                            last.then_inc(proj_ps, 1)

                        for s in range(2 * HEADS):
                            if "now" in on:
                                scores_T(s)
                            if "maxima" in on:
                                scores(s)
                            if s in (6, 10, 14) and "now" in on:
                                values(s // 4 - 1, it, b)
                            if s == 2 and "tail" in on:
                                values(3, it - 1, b3)
                            if s == 5 and "tail" in on:
                                turn(1, it - 1)
                            if s == 13 and "now" in on:
                                turn(0, it)
                            if s == 1 and bank("mT1"):
                                max_T(1, it)
                            if s == 2 and "tail" in on:
                                proj(0, it - 1)
                            if s == 2 and bank("yT"):
                                pe.wait_ge(y_ready, it + 4)
                                for t in range(4):
                                    last = pe.transpose(ps[:, 7, t * R:(t + 1) * R], y[:, t, :], ident[0:R, 0:R])
                                last.then_inc(yT_ps, 1)
                            if s in (4, 6) and bank("q" if s == 4 else "k"):
                                i = 0 if s == 4 else 1
                                pe.wait_ge(yT_ready, it + 4)
                                pe.matmul(ps[:, 7, 0:W2], wqkv[:, i * D:(i + 1) * D], yT[:, :], start=True, stop=True).then_inc(qk_ps, 1)
                            if s == 9 and bank("mT0"):
                                max_T(0, it + 1)
                            if s == 10 and bank("oT1"):
                                out_T(1, it - 1)
                            if s == 11 and "tail" in on:
                                proj(1, it - 1)
                            if s == 12 and bank("v"):
                                for t in range(4):
                                    last = pe.matmul(ps[0:R, 7, t * D:(t + 1) * D], yT[:, t * R:(t + 1) * R], wqkv[:, 2 * D:3 * D], start=True, stop=True)
                                last.then_inc(v_ps, 1)
                            if s == 15 and bank("oT0"):
                                out_T(0, it)
                    slots(pe, l, body)

                    def transposes(p, b):
                        n = l * PAIRS + p
                        pe.wait_ge(z_ready, n + 1)
                        if type(p) is not int or p >= 2:
                            pe.wait_ge(zT_ready, n - 1)
                        for t in range(4):
                            last = pe.transpose(ps[:, b % 2, t * R:(t + 1) * R], z[:, b, t, :], ident[0:R, 0:R])
                        last.then_inc(zT_ps, 1)

                    def up(p, b):
                        n = l * PAIRS + p
                        pe.wait_ge(zT_ready, n + 1)
                        if type(p) is not int or p >= 2:
                            pe.wait_ge(hid_ready, n - 1)
                        for c in range(2):
                            last = pe.matmul(ps[:, 2 + 2 * b + c, 0:W2], wfc1[:, c * D:(c + 1) * D], zT[:, b, :], start=True, stop=True)
                        last.then_inc(hid_ps, 1)

                    def down(p, b):
                        n = l * PAIRS + p
                        pe.wait_ge(hid_ready, n + 1)
                        if type(p) is not int or p >= 2:
                            pe.wait_ge(mlp_done, n - 1)
                        else:
                            pe.wait_ge(attn_done, l * (2 * PAIRS) + 2 * PAIRS)
                        for t in range(4):
                            for c in range(2):
                                last = pe.matmul(ps[0:R, 6 + b, t * D:(t + 1) * D], hid[:, b, c, t * R:(t + 1) * R], wfc2[:, c, :],
                                                 start=(c == 0), stop=(c == 1))
                        last.then_inc(fc2_ps, 1)

                    transposes(0, 0)
                    transposes(1, 1)
                    up(0, 0)

                    def four(q):
                        for u in range(4):
                            transposes(q * 4 + (2 + u), (2 + u) % 4)
                            up(q * 4 + (1 + u), (1 + u) % 2)
                            down(q * 4 + u, u % 2)
                    four(0)
                    with pe.Fori(0, PAIRS // 4 - 2) as q:
                        four(q + 1)
                    for p in range(PAIRS - 4, PAIRS):
                        if p + 2 < PAIRS:
                            transposes(p + 2, (p + 2) % 4)
                        if p + 1 < PAIRS:
                            up(p + 1, (p + 1) % 2)
                        down(p, p % 2)

            @block.vector
            def _(dve):
                def statistics(pair, n, s_stats, s_aggr, s_used):
                    dve.wait_ge(s_used, n)
                    dve.sem_inc(passed, 1)
                    for t in range(4):
                        last = dve.bn_stats(stats[:, t, :], h[:, bass.ds(pair * 4 + t, 1), :].rearrange("p a d -> p (a d)"))
                    last.then_inc(s_stats, 1)

                def aggregate(n, s_stats, s_aggr):
                    dve.wait_ge(s_stats, n + 1)
                    dve.sem_inc(passed, 1)
                    for t in range(4):
                        last = dve.bn_aggr(mv[:, t, :], stats[:, t, :])
                    last.then_inc(s_aggr, 1)

                with dve.Fori(0, DEPTH) as l:
                    dve.wait_ge(raw_in, (l + 1) * RAW)
                    dve.wait_ge(fc2_ps, l * PAIRS)
                    dve.wait_ge(hbias2, l * PAIRS)
                    dve.wait_ge(mlp_done, l * PAIRS)
                    dve.tensor_scalar(wqkv[:, :], wqkv_raw[:, :], cols[:, 0:1], None, ALU.mult)
                    dve.tensor_scalar(wfc1[:, :], wfc1_raw[:, :], cols[:, 2:3], None, ALU.mult)
                    dve.tensor_copy(wproj[:, :], wproj_raw[:, :])
                    dve.tensor_copy(wfc2[:, :, :], wfc2_raw[:, :, :])
                    dve.wait_ge(prep_mm, l * 2 + 1)
                    dve.tensor_tensor(bfc1[:, :], ps[:, 0, 3:5], fc1b[:, :], ALU.add)
                    dve.tensor_tensor(bqkv[:, :], ps[:, 0, 0:3], qkvb[:, :], ALU.add).then_inc(bias_ready, 1)
                    dve.wait_ge(bias_ready, l + 1)
                    dve.tensor_copy(bv_wide[:, :], bqkv[:, 2:3].to_broadcast([128, R])).then_inc(bvw_ready, 1)
                    dve.wait_ge(prep_mm, l * 2 + 2)
                    dve.tensor_copy(bfc2[:, :], ps[0:R, 2, 0:D])
                    dve.tensor_copy(bproj[:, :], ps[0:R, 1, 0:D]).then_inc(weights_ready, 1)

                    def body(k, b, on):
                        it = l * PAIRS + k

                        def row_max(s):
                            if "maxima" not in on:
                                return
                            im, hd = s // HEADS, s % HEADS
                            n = it + 1
                            dve.wait_ge(mx_ps, n * 16 + (s + 1))
                            if hd == 0 and (type(k) is not int or k > -1):
                                dve.wait_ge(mT_ps, n * 2 + (im - 1))
                            dve.tensor_reduce(negmax[:, im, :, hd], ps[0:R, 4 + s % 2, 0:2 * W].rearrange("p (t c) -> p t c", t=2),
                                              AX.X, ALU.max, negate=True).then_inc(mx_done, 1)

                        def max_low(im, pair, stage):
                            if stage in on:
                                n = pair * 2 + im
                                dve.wait_ge(mhi_ready, n + 1)
                                dve.tensor_tensor(mlo[:, im, :], ps[0:2 * HEADS, 7, 0:R], mhi[:, im, :], ALU.subtract).then_inc(mlo_ready, 1)

                        def remainder(i):
                            if "project" in on:
                                dve.wait_ge(part1, it * 2 + (6 + i + 1))
                                dve.scalar_tensor_tensor(rest[:, i, :], ps[:, 7, 0:W2], bqkv[:, i:i + 1], parts[:, i, 0, :],
                                                         ALU.add, ALU.subtract).then_inc(rest_ready, 1)

                        def normalise(im, pair, stage):
                            if stage in on:
                                n = pair * 2 + im
                                dve.wait_ge(oU_turned, n + 1)
                                heads = ps[0:R, 3, :].rearrange("p (h v) -> p h v", v=32)
                                dve.reciprocal(rsum[:, :], heads[:, :, HD]).then_inc(rsum_ready, 1)
                                dve.wait_ge(oT_ps, n)
                                dve.wait_ge(rsum_ready, n + 1)
                                dve.tensor_tensor(o[:, :, :].rearrange("p t (h d) -> p (t h) d", h=HEADS), heads[:, :, 0:HD],
                                                  rsum[:, :].rearrange("p (h a) -> p h a", a=1).to_broadcast([R, 2 * HEADS, HD]),
                                                  ALU.mult).then_inc(o_ready, 1)

                        def residual(im, pair, pair_in_layer, stage):
                            if stage in on:
                                dve.wait_ge(proj_ps, pair * 2 + (im + 1))
                                dve.wait_ge(hbias, pair + 1)
                                hi = h[:, bass.ds(pair_in_layer * 4 + 2 * im, 2), :]
                                dve.tensor_tensor(hi, ps[0:R, 3, 0:2 * D].rearrange("p (t d) -> p t d", t=2), hi, ALU.add).then_inc(attn_done, 1)

                        for s in range(2 * HEADS):
                            row_max(s)
                            if s == 0 and "norm" in on:
                                dve.wait_ge(ln_centred, it + 4)
                                aggregate(it + 4, ln_stats, ln_aggr)
                            if s == 2:
                                max_low(1, it, "now")
                            if s == 3:
                                residual(0, it - 1, k - 1, "tail")
                            if s == 5:
                                remainder(0)
                            if s == 6:
                                normalise(1, it - 1, "tail")
                            if s == 7:
                                remainder(1)
                            if s == 9:
                                max_low(0, it + 1, "maxima")
                            if s == 12:
                                residual(1, it - 1, k - 1, "tail")
                            if s == 14:
                                normalise(0, it, "now")
                            if s == 15 and "stats" in on:
                                statistics(k + 5, it + 5, ln_stats, ln_aggr, ln_aggr)
                    slots(dve, l, body)

                    def mlp_residual(p, b):
                        n = l * PAIRS + p
                        dve.wait_ge(fc2_ps, n + 1)
                        dve.wait_ge(hbias2, n + 1)
                        hp = h[:, bass.ds(p * 4, 4), :]
                        dve.tensor_tensor(hp, ps[0:R, 6 + b, :].rearrange("p (t d) -> p t d", t=4), hp, ALU.add).then_inc(mlp_done, 1)

                    def mlp_statistics(p, b):
                        n = l * PAIRS + p
                        dve.wait_ge(attn_done, n * 2 + 2)
                        statistics(p, n, ln2_stats, ln2_aggr, ln2_aggr)
                        dve.wait_ge(ln2_stats, n + 1)
                        if type(p) is not int or p >= NZ:
                            dve.wait_ge(z_ready, n - (NZ - 1))
                        dve.sem_inc(passed, 1)
                        for t in range(4):
                            last = dve.bn_aggr(mv2[:, b, t, :], stats[:, t, :])
                        last.then_inc(ln2_aggr, 1)

                    def mlp_norm(p, b):
                        n = l * PAIRS + p
                        dve.wait_ge(ln2_rstd, n + 1)
                        if type(p) is not int or p >= NZ:
                            dve.wait_ge(zT_ps, n - (NZ - 1))
                        for t in range(4):
                            last = dve.tensor_scalar(z[:, b, t, :], h[:, bass.ds(p * 4 + t, 1), :].rearrange("p a d -> p (a d)"),
                                                     mv2[:, b, t, 0:1], rstd2[:, b, t:t + 1], ALU.subtract, ALU.mult)
                        last.then_inc(z_ready, 1)

                    mlp_statistics(0, 0)
                    mlp_statistics(1, 1)
                    for p in range(3):
                        mlp_norm(p, p % NZ)
                        mlp_statistics(p + 2, (p + 2) % NZ)

                    def step(p, u):
                        mlp_norm(p + 3, (u + 3) % NZ)
                        mlp_statistics(p + 5, (u + 5) % NZ)
                        mlp_residual(p, u % 2)
                    with dve.Fori(0, (PAIRS - 5) // NZ) as q:
                        for u in range(NZ):
                            step(q * NZ + u, u)
                    for p in range((PAIRS - 5) // NZ * NZ, PAIRS):
                        if p + 3 < PAIRS:
                            mlp_norm(p + 3, (p + 3) % NZ)
                        if p + 5 < PAIRS:
                            mlp_statistics(p + 5, (p + 5) % NZ)
                        mlp_residual(p, p % 2)

        EXPERTS = A["Wr"].shape[1]
        GW = D + EXPERTS
        table = nc.dram_tensor("table", [IMAGES, NTOK, GW], f32, kind="Internal").ap()
        sb, pb, sem = scope_tools(top)
        logits = sb("logits", [R, TILES, EXPERTS])
        with ExitStack() as st:
            sb, pb, sem = scope_tools(st)
            UW = D + 1
            NU = 4
            neghalf = sb("r_neghalf", [128, 128])
            eps_t = sb("r_eps_t", [R, 3, 4])
            mhalf = sb("r_mhalf", [R, 3, 4])
            wnorm = sb("r_wnorm", [R, D])
            bnorm = sb("r_bnorm", [R, D])
            wr = sb("r_wr", [128, EXPERTS])
            stats = sb("r_stats", [R, 3, 4, 6])
            mv = sb("r_mv", [R, 2, 3, 4, 2])
            var = sb("r_var", [R, 3, 4])
            rstd = sb("r_rstd", [R, 2, 3, 4])
            yn = sb("r_yn", [R, 2, 4, D])
            yw = sb("r_yw", [R, 4, D])
            u = sb("r_u", [R, NU, 4, UW])
            square = sb("r_square", [R, 4, D])
            sqsum = sb("r_sqsum", [R, NU, 4])
            nsq = sb("r_nsq", [R, NU, 4])
            uT = sb("r_uT", [128, 2, W2])
            uT2 = sb("r_uT2", [128, 2, W2])
            dist = sb("r_dist", [R, 2, 2, W])
            kern = sb("r_kern", [R, 2, 2 * W])
            prob = sb("r_prob", [R, 2, 2, 2 * W])
            rden = sb("r_rden", [R, 4])
            xc = sb("r_xc", [R, 4, D])
            g = sb("r_g", [R, 2, 4, D])
            gT = sb("r_gT", [128, W2])
            ps = pb("r_ps", [128, 8, 512])

            mv_ready, var_ready, rstd_ready, applied = (sem("r_" + n) for n in ("mv_ready", "var_ready", "rstd_ready", "applied"))
            consts, rows_in, st_ready, yn_ready, weighted, normed, u_ready, sq_ready, nsq_ready = (sem("r_" + n) for n in (
                "consts", "rows_in", "st_ready", "yn_ready", "weighted", "normed", "u_ready", "sq_ready", "nsq_ready"))
            uT_ps, uT_ready, uT2_ready, dots_ps, dist_ready, kern_ready, prob_ready, attn_ps, rden_ready, h_done = (sem("r_" + n) for n in (
                "uT_ps", "uT_ready", "uT2_ready", "dots_ps", "dist_ready", "kern_ready", "prob_ready", "attn_ps", "rden_ready", "h_done"))
            g_ready, gT_ps, gT_ready, logit_ps, logit_done, h_saved = (sem("r_" + n) for n in (
                "g_ready", "gT_ps", "gT_ready", "logit_ps", "logit_done", "h_saved"))
            g_saved = [sem("r_g_saved0"), sem("r_g_saved1")]
            centred = sem("r_centred")
            block = st.enter_context(nc.Block())

            LAGS = {"norm_stats": 8, "norm": 7, "unit_stats": 6, "unit": 5, "turn": 4, "kernel": 3, "mix": 2,
                    "final_stats": 1, "final": 0, "route": -1}
            LNS = (("norm", 0), ("unit", 1), ("final", 2))
            FIRST = -8

            def slots(engine, body):
                def on(k):
                    return {n for n, lag in LAGS.items() if 0 <= k + lag < PAIRS}
                for k in range(FIRST, 1):
                    body(k, k % 4, on(k))
                loops = (PAIRS - 9) // 4
                with engine.Fori(0, loops) as q:
                    for j in range(4):
                        body(q * 4 + (j + 1), (j + 1) % 4, on(1))
                for k in range(loops * 4 + 1, PAIRS + 1):
                    body(k, k % 4, on(k))

            def wait(engine, s, n):
                if type(n) is not int or n > 0:
                    engine.wait_ge(s, n)

            @block.sync
            def _(sp):
                sp.dma_start(wnorm[:, :], A["norm_w"].partition_broadcast(R)).then_inc(rows_in, 16)
                sp.dma_start(bnorm[:, :], A["norm_b"].partition_broadcast(R)).then_inc(rows_in, 16)
                sp.dma_start(wr[:, :], A["Wr"]).then_inc(rows_in, 16)

                def save(dst, src, s):
                    sp.dma_start(dst[0, 1:NTOK, :].rearrange("(t p) d -> p t d", p=P1), src[0:P1, :, :]).then_inc(s, 16)
                    sp.dma_start(dst[0, 0:1, :], src[P1:R, 0, :]).then_inc(s, 16)

                def body(k, j, on):
                    if "mix" in on:
                        sp.wait_ge(h_done, k + 3)
                        for im in range(2):
                            save(out[bass.ds(k * 2 + (4 + im), 1)], h[:, bass.ds(k * 4 + (8 + 2 * im), 2), :], h_saved)
                    if "final" in on:
                        sp.wait_ge(g_ready, k + 1)
                        for im in range(2):
                            save(table[bass.ds(k * 2 + im, 1), :, 0:D], g[:, j % 2, 2 * im:2 * im + 2, :], g_saved[j % 2])
                slots(sp, body)
                sp.wait_ge(h_saved, IMAGES * 32)
                for i in range(2):
                    sp.wait_ge(g_saved[i], IMAGES * 16)

            @block.gpsimd
            def _(pool):
                pool.memset(neghalf[:, :], -0.5)
                pool.memset(eps_t[:, :, :], EPS)
                pool.memset(mhalf[:, :, :], -0.5)
                pool.memset(mv[:, :, :, :, :], 1.0)
                pool.memset(u[:, :, :, :], 1.0).then_inc(consts, 1)
                pool.wait_ge(consts, 1)
                pool.wait_ge(rows_in, 48)

                def wide(row):
                    return row[:, :].rearrange("p (a d) -> p a d", a=1).to_broadcast([R, 4, D])

                def body(k, j, on):
                    if "final" in on:
                        wait(pool, g_ready, k)
                        wait(pool, rstd_ready, k - FIRST)
                        pool.sem_inc(passed, 1)
                        pool.tensor_tensor(xc[:, :, :], h[:, bass.ds(k * 4, 4), :], mv[:, (j + 1) % 2, 2, :, 0:1].to_broadcast([R, 4, D]),
                                           ALU.subtract).then_inc(centred, 1)
                        wait(pool, g_saved[j % 2], (k - j % 2) * 32)
                        wait(pool, gT_ps, k - 1)
                        pool.wait_ge(centred, k + 1)
                        pool.tensor_tensor(g[:, j % 2, :, :], xc[:, :, :], rstd[:, (j + 1) % 2, 2, :].rearrange("p (t a) -> p t a", a=1)
                                           .to_broadcast([R, 4, D]), ALU.mult).then_inc(g_ready, 1)
                    if "norm" in on:
                        n = k + 7
                        wait(pool, normed, n)
                        pool.wait_ge(yn_ready, n + 1)
                        pool.tensor_tensor(yw[:, :, :], yn[:, (j + 1) % 2, :, :], wide(wnorm), ALU.mult).then_inc(weighted, 1)
                        pool.wait_ge(weighted, n + 1)
                        pool.sem_inc(passed, 1)
                        pool.tensor_tensor(h[:, bass.ds(n * 4, 4), :], yw[:, :, :], wide(bnorm), ALU.add).then_inc(normed, 1)
                    if "unit" in on:
                        n = k + 5
                        pool.wait_ge(sq_ready, n + 1)
                        wait(pool, dist_ready, n * 2 - 6)
                        pool.tensor_tensor(nsq[:, (j + 1) % 4, :], sqsum[:, (j + 1) % 4, :], mhalf[:, 0, :], ALU.mult).then_inc(nsq_ready, 1)
                    if {"norm_stats", "unit_stats", "final_stats"} & on:
                        n = k - FIRST + 1
                        wait(pool, rstd_ready, n - 1)
                        pool.wait_ge(mv_ready, n)
                        pool.tensor_tensor(var[:, :, :], mv[:, j % 2, :, :, 1], eps_t[:, :, :], ALU.add).then_inc(var_ready, 1)
                        wait(pool, applied, n - 2)
                        wait(pool, g_ready, k)
                        pool.wait_ge(var_ready, n)
                        pool.tensor_tensor(rstd[:, j % 2, :, :], var[:, :, :], mhalf[:, :, :], ALU.pow).then_inc(rstd_ready, 1)
                slots(pool, body)

            @block.scalar
            def _(act):
                def body(k, j, on):
                    if "route" in on:
                        act.wait_ge(gT_ps, k)
                        wait(act, logit_ps, k - 1)
                        act.activation(gT[:, :], ps[:, 6, 0:W2], ACT.Copy).then_inc(gT_ready, 1)
                    if "kernel" in on:
                        for im in range(2):
                            n = k * 2 + (6 + im)
                            act.wait_ge(dist_ready, n + 1)
                            wait(act, prob_ready, n - 1)
                            act.activation(kern[:, im, :], dist[:, im, :, :].rearrange("p t c -> p (t c)"), ACT.Exp, scale=2.0).then_inc(kern_ready, 1)
                    if "turn" in on:
                        n = k + 4
                        act.wait_ge(uT_ps, n + 1)
                        wait(act, dots_ps, n * 2 - 2)
                        act.activation(uT[:, j % 2, :], ps[:, 0, 0:W2], ACT.Copy).then_inc(uT_ready, 1)
                        act.activation(uT2[:, j % 2, :], ps[:, 0, 0:W2], ACT.Square).then_inc(uT2_ready, 1)
                    if "kernel" in on:
                        for im in range(2):
                            n = k * 2 + (6 + im)
                            act.wait_ge(kern_ready, n + 1)
                            wait(act, attn_ps, n - 3)
                            act.activation(prob[:, (j + 1) % 2, im, :], kern[:, im, :], ACT.Exp).then_inc(prob_ready, 1)
                    if "unit" in on:
                        n = k + 5
                        act.wait_ge(u_ready, n + 1)
                        wait(act, nsq_ready, n - 3)
                        wait(act, sq_ready, n)
                        for t in range(4):
                            last = act.activation(square[:, t, :], u[:, (j + 1) % 4, t, 0:D], ACT.Square, accum_out=sqsum[:, (j + 1) % 4, t:t + 1])
                        last.then_inc(sq_ready, 1)
                slots(act, body)

            @block.tensor
            def _(pe):
                pe.wait_ge(consts, 1)
                pe.wait_ge(rows_in, 48)

                def body(k, j, on):
                    if "route" in on:
                        pe.wait_ge(g_ready, k)
                        wait(pe, gT_ready, k - 1)
                        for t in range(4):
                            last = pe.transpose(ps[:, 6, t * R:(t + 1) * R], g[:, (j + 1) % 2, t, :], ident[0:R, 0:R])
                        last.then_inc(gT_ps, 1)
                    if "kernel" in on:
                        n = k + 3
                        b = (j + 1) % 2
                        pe.wait_ge(uT2_ready, n + 1)
                        pe.wait_ge(uT_ready, n + 1)
                        for im in range(2):
                            wait(pe, dist_ready, n * 2 + (im - 1))
                            for t in range(2):
                                dst = ps[0:R, 2 + im, t * W:(t + 1) * W]
                                pe.matmul(dst, uT[:, b, im * W + t * R:im * W + (t + 1) * R], uT[:, b, im * W:(im + 1) * W], start=True, stop=False)
                                last = pe.matmul(dst, neghalf[:, 0:R], uT2[:, b, im * W:(im + 1) * W], start=False, stop=True)
                            last.then_inc(dots_ps, 1)
                    if "route" in on:
                        pe.wait_ge(gT_ready, k)
                        wait(pe, logit_done, k - 1)
                        for t in range(4):
                            last = pe.matmul(ps[0:R, 7, t * EXPERTS:(t + 1) * EXPERTS], gT[:, t * R:(t + 1) * R], wr[:, :], start=True, stop=True)
                        last.then_inc(logit_ps, 1)
                    if "turn" in on:
                        n = k + 4
                        pe.wait_ge(u_ready, n + 1)
                        wait(pe, uT2_ready, n)
                        for t in range(4):
                            last = pe.transpose(ps[:, 0, t * R:(t + 1) * R], u[:, j % 4, t, 0:D], ident[0:R, 0:R])
                        last.then_inc(uT_ps, 1)
                    if "mix" in on:
                        n = k + 2
                        for im in range(2):
                            pe.wait_ge(prob_ready, n * 2 + (im + 1))
                            wait(pe, h_done, n)
                            for tq in range(2):
                                for tk, rows_k in ((0, R), (1, P1)):
                                    last = pe.matmul(ps[0:R, 4 + im, tq * UW:(tq + 1) * UW], prob[0:rows_k, j % 2, im, tk * W + tq * R:tk * W + (tq + 1) * R],
                                                     u[0:rows_k, (j + 2) % 4, 2 * im + tk, :], start=(tk == 0), stop=(tk == 1))
                            last.then_inc(attn_ps, 1)
                slots(pe, body)

            @block.vector
            def _(dve):
                dve.wait_ge(consts, 1)

                def body(k, j, on):
                    slot = k - FIRST + 1
                    lns = [(name, i) for name, i in LNS if name + "_stats" in on]
                    if lns:
                        wait(dve, mv_ready, slot - 1)
                        if "unit_stats" in on:
                            wait(dve, normed, k + 7)
                        if "final_stats" in on:
                            dve.wait_ge(h_done, k + 2)
                        dve.sem_inc(passed, 1)
                        for name, i in lns:
                            for t in range(4):
                                last = dve.bn_stats(stats[:, i, t, :], h[:, bass.ds(k * 4 + (4 * LAGS[name + "_stats"] + t), 1), :].rearrange("p a d -> p (a d)"))
                        last.then_inc(st_ready, 1)
                    if "kernel" in on:
                        n = k + 3
                        dve.wait_ge(nsq_ready, n + 1)
                        for im in range(2):
                            dve.wait_ge(dots_ps, n * 2 + (im + 1))
                            wait(dve, kern_ready, n * 2 + (im - 1))
                            for t in range(2):
                                last = dve.tensor_scalar(dist[:, im, t, :], ps[0:R, 2 + im, t * W:(t + 1) * W],
                                                         nsq[:, (j + 3) % 4, 2 * im + t:2 * im + t + 1], 0.0, ALU.add, ALU.min)
                            last.then_inc(dist_ready, 1)
                    applies = [(name, i) for name, i in LNS[:2] if name in on]
                    if applies:
                        dve.wait_ge(rstd_ready, slot - 1)

                    for name, i in applies:
                        n = k + LAGS[name]
                        if name == "norm":
                            wait(dve, weighted, n - 1)
                            dst, done = yn[:, (j + 1) % 2, :, :], yn_ready
                        else:
                            wait(dve, attn_ps, n * 2 - 6)
                            wait(dve, sq_ready, n - 3)
                            dst, done = u[:, (j + 1) % 4, :, 0:D], u_ready
                        for t in range(4):
                            last = dve.tensor_scalar(dst[:, t, :], h[:, bass.ds(n * 4 + t, 1), :].rearrange("p a d -> p (a d)"),
                                                     mv[:, (j + 1) % 2, i, t, 0:1], rstd[:, (j + 1) % 2, i, t:t + 1], ALU.subtract, ALU.mult)
                        last.then_inc(done, 1)
                    if applies:
                        dve.wait_ge(done, k + LAGS[applies[-1][0]] + 1)
                    if type(k) is not int or k > FIRST:
                        dve.sem_inc(applied, 1)
                    if lns:
                        dve.wait_ge(st_ready, slot)
                        wait(dve, applied, slot - 2)
                        wait(dve, centred, k)
                        dve.sem_inc(passed, 1)
                        for name, i in lns:
                            for t in range(4):
                                last = dve.bn_aggr(mv[:, j % 2, i, t, :], stats[:, i, t, :])
                        last.then_inc(mv_ready, 1)
                    if "route" in on:
                        dve.wait_ge(logit_ps, k)
                        dve.sem_inc(passed, 1)
                        dve.tensor_copy(logits[:, bass.ds(k * 4 - 4, 4), :], ps[0:R, 7, 0:4 * EXPERTS].rearrange("p (t e) -> p t e", t=4)).then_inc(logit_done, 1)
                    if "mix" in on:
                        n = k + 2
                        for im in range(2):
                            dve.wait_ge(attn_ps, n * 2 + (im + 1))
                            outs = ps[0:R, 4 + im, 0:2 * UW].rearrange("p (t d) -> p t d", t=2)
                            dve.reciprocal(rden[:, 2 * im:2 * im + 2], outs[:, :, D]).then_inc(rden_ready, 1)
                            dve.wait_ge(rden_ready, n * 2 + (im + 1))
                            for t in range(2):
                                hi = h[:, bass.ds(n * 4 + (2 * im + t), 1), :].rearrange("p a d -> p (a d)")
                                last = dve.scalar_tensor_tensor(hi, outs[:, t, 0:D], rden[:, 2 * im + t:2 * im + t + 1], hi, ALU.mult, ALU.add)
                        last.then_inc(h_done, 1)
                slots(dve, body)

        CAP = 1024
        F = A["W1"].shape[2]
        FC = F // 128
        E8 = EXPERTS
        TB = TILES // (128 // E8)
        LO, HI = 64, CAP // 64
        EH = 2
        SL = CAP // 128
        table_rows = table.rearrange("b n w -> (b n) w")
        out_rows = out.rearrange("b n d -> (b n) d")
        sb, pb, sem = scope_tools(top)
        index_all = sb("index_all", [128, E8, SL], i32)
        with ExitStack() as st:
            sb, pb, sem = scope_tools(st)
            dup = sb("dup", [R, 2])
            dup1 = sb("dup1", [R, 2])
            fold = sb("fold", [128, E8])
            same = sb("same", [128, 128])
            before = sb("before", [R, R], bf16)
            onesb = sb("onesb", [R, 128], bf16)
            iota_n = sb("iota_n", [R, 2], i32)
            iota_b = sb("iota_b", [R, IMAGES], i32)
            n_f = sb("n_f", [R, 2])
            nval = sb("nval", [R, IMAGES, 2], bf16)
            bval = sb("bval", [R, IMAGES, 2], bf16)
            colmax = sb("colmax", [128, 1])
            negmax8 = sb("negmax8", [1, E8])
            row = sb("row", [1, 128])
            nmax = sb("nmax", [128, 1])
            esum = sb("esum", [128, 1])
            rsum = sb("rsum8", [128, 1])
            expd = sb("expd", [128, TB * R])
            pT = sb("pT", [128, TB * R])
            over = sb("over", [128, TB * R])
            pm = sb("pm", [R, TILES, E8])
            cand = sb("cand", [128, 1])
            low = sb("low", [128, 1])
            step = sb("step", [128, 1])
            count = sb("count", [128, 1])
            flag = sb("flag", [128, 1])
            row8 = sb("row8", [1, E8])
            thr = sb("thr", [R, E8])
            above = sb("above", [R, TILES, E8], bf16)
            equal = sb("equal", [R, TILES, E8], bf16)
            chosen = sb("chosen", [R, TILES, E8], bf16)
            running = sb("running", [R, TILES, E8])
            rank = sb("rank", [R, TILES, E8])
            taken = sb("taken", [R, E8])
            room = sb("room", [R, E8])
            slot_i = sb("slot_i", [R, TILES, E8], i32)
            slot_h = sb("slot_h", [R, TILES, E8], i32)
            lo_b = sb("lo_b", [R, E8, TILES], bf16)
            hi_b = sb("hi_b", [R, E8, TILES], bf16)
            lo_hot = sb("lo_hot", [R, EH, LO, TILES], bf16)
            hi_hot = sb("hi_hot", [R, HI, EH, TILES], bf16)
            hi_val = sb("hi_val", [R, 2, HI, EH, TILES], bf16)
            tok_b = sb("tok_b", [128, HI])
            index = sb("index", [128, 2, E8 // EH, SL], i32)
            ps = pb("moe_ps", [128, 8, 512])
            ps_flat = ps[:, :, :].rearrange("p a b -> p (a b)")

            setup, ready, turned = sem("setup"), sem("ready"), sem("turned")
            dve_n, pe_n, exp_done, p_saved, idx_moved = sem("dve_n"), sem("pe_n"), sem("exp_done"), sem("p_saved"), sem("idx_moved")
            cand_ready, counted, total, flagged, hot_ready, idx_ps, idx_read = (sem(n) for n in (
                "cand_ready", "counted", "total", "flagged", "hot_ready", "idx_ps", "idx_read"))
            hi_ready, image_ready = sem("hi_ready"), sem("image_ready")
            block = st.enter_context(nc.Block())

            STEPS = ["masked", "colmax", "negmax", "row", "nmax", "rsum", "pT", "pm_raw", "pm", "low0"]
            AT = {n: i + 1 for i, n in enumerate(STEPS)}

            @block.gpsimd
            def _(pool):
                def put(ins, n):
                    ins.then_inc(setup, 1)
                    pool.wait_ge(setup, n)
                put(pool.memset(dup[:, :], 0.0), 1)
                put(pool.affine_select(out=dup[:, 1:2], in_=dup[:, 1:2], compare_op=ALU.not_equal, fill=-3.0e38, base=-P1,
                                       pattern=[[0, 1]], channel_multiplier=1), 2)
                put(pool.memset(dup1[:, :], 0.0), 3)
                put(pool.affine_select(out=dup1[:, 1:2], in_=dup1[:, 1:2], compare_op=ALU.not_equal, fill=-1.0, base=-P1,
                                       pattern=[[0, 1]], channel_multiplier=1), 4)
                put(pool.memset(onesb[:, :], 1.0), 5)
                put(pool.memset(before[:, 0:P1], 1.0), 6)
                put(pool.memset(before[:, P1:R], 0.0), 7)
                put(pool.affine_select(out=before[:, 0:P1], in_=before[:, 0:P1], compare_op=ALU.is_gt, fill=0.0, base=0,
                                       pattern=[[1, P1]], channel_multiplier=-1), 8)
                put(pool.affine_select(out=before[:, 0:P1], in_=before[:, 0:P1], compare_op=ALU.not_equal, fill=1.0, base=-P1,
                                       pattern=[[0, P1]], channel_multiplier=1), 9)
                put(pool.iota(iota_n[:, :], pattern=[[P1, 2]], base=1, channel_multiplier=1), 10)
                put(pool.iota(iota_b[:, :], pattern=[[1, IMAGES]], base=0, channel_multiplier=0), 11)
                put(pool.tensor_copy(n_f[:, :], iota_n[:, :]), 12)
                put(pool.affine_select(out=n_f[:, :], in_=n_f[:, :], compare_op=ALU.not_equal, fill=0.0, base=-P1,
                                       pattern=[[0, 2]], channel_multiplier=1), 13)
                pool.tensor_copy(nval[:, :, :], n_f[:, :].rearrange("p (a t) -> p a t", a=1).to_broadcast([R, IMAGES, 2])).then_inc(setup, 1)
                pool.tensor_copy(bval[:, :, :], iota_b[:, :].rearrange("p (b a) -> p b a", a=1).to_broadcast([R, IMAGES, 2])).then_inc(setup, 1)
            SETUP = 15

            @block.sync
            def _(sp):
                sp.wait_ge(dve_n, AT["pm"])
                for t in range(2):
                    sp.dma_start(table[:, 1 + t * P1:1 + (t + 1) * P1, D:GW].rearrange("b p e -> p b e"),
                                 pm[0:P1, :, :].rearrange("p (b t) e -> p b t e", t=2)[:, :, t, :]).then_inc(p_saved, 16)
                sp.dma_start(table[:, 0:1, D:GW].rearrange("b p e -> p b e"),
                             pm[P1:R, :, :].rearrange("p (b t) e -> p b t e", t=2)[:, :, 0, :]).then_inc(p_saved, 16)
                sp.wait_ge(idx_read, E8 // EH)
                for e in range(EH):
                    sp.dma_start(index_all[(1 - e) * LO:(2 - e) * LO, :, :].rearrange("p (c e) s -> p c e s", e=EH)[:, :, e, :],
                                 index[e * LO:(e + 1) * LO, 1 - e, :, :]).then_inc(idx_moved, 16)
                sp.wait_ge(idx_moved, 32)
                sp.wait_ge(p_saved, 48)

            @block.scalar
            def _(act):
                act.wait_ge(dve_n, AT["nmax"])
                act.activation(expd[:, :].rearrange("p (a b) -> p a b", a=2), ps[:, 0:2, 0:TB * R // 2], ACT.Exp, bias=nmax[:, 0:1],
                               accum_out=esum[:, 0:1]).then_inc(exp_done, 1)

            MANTISSA = 23

            @block.tensor
            def _(pe):
                pe.wait_ge(dve_n, AT["masked"])
                for i in range(TB):
                    last = pe.transpose(ps[:, i // 4, (i % 4) * R:(i % 4 + 1) * R],
                                        logits[:, 16 * i:16 * (i + 1), :].rearrange("p t e -> p (t e)"), ident[0:R, 0:R])
                last.then_inc(pe_n, 1)
                pe.wait_ge(dve_n, AT["colmax"])
                pe.transpose(ps[0:1, 2, 0:128], colmax[:, 0:1], ident[:, :]).then_inc(pe_n, 1)
                pe.wait_ge(dve_n, AT["row"])
                pe.matmul(ps[:, 3, 0:1], row[0:1, :], ones[0:1, 0:1], start=True, stop=True).then_inc(pe_n, 1)
                pe.wait_ge(exp_done, 1)
                pe.matmul(ps[:, 2, 0:1], same[:, :], esum[:, 0:1], start=True, stop=True).then_inc(pe_n, 1)
                pe.wait_ge(dve_n, AT["pT"])
                for i in range(TB):
                    last = pe.transpose(ps[0:R, 4 + i // 4, (i % 4) * 128:(i % 4 + 1) * 128], pT[:, i * R:(i + 1) * R], ident[:, :])
                last.then_inc(pe_n, 1)

                def sum_up(n):
                    pe.wait_ge(counted, n)
                    pe.matmul(ps[:, 6, 0:1], same[:, :], count[:, 0:1], start=True, stop=True).then_inc(total, 1)
                for n in range(7):
                    sum_up(n + 1)
                with pe.Fori(0, MANTISSA) as i:
                    sum_up(i + 8)
                sum_up(7 + MANTISSA + 1)
                pe.wait_ge(ready, 1)
                pe.transpose(ps[0:1, 7, 0:128], low[:, 0:1], ident[:, :]).then_inc(turned, 1)
                pe.wait_ge(ready, 2)
                pe.matmul(ps[0:R, 6, 0:E8], ones[0:1, 0:R], row8[0:1, :], start=True, stop=True).then_inc(turned, 1)

                def prefix(mask, bank_prefix, bank_total):
                    m = mask[:, :, :].rearrange("p t e -> p (t e)")
                    for i in range(2):
                        if bank_prefix is not None:
                            pe.matmul(ps[0:R, bank_prefix + i, :], before[:, :], m[:, i * 512:(i + 1) * 512], start=True, stop=True)
                        last = pe.matmul(ps[0:R, bank_total + i, :], onesb[:, 0:R], m[:, i * 512:(i + 1) * 512], start=True, stop=True)
                    last.then_inc(turned, 1)
                pe.wait_ge(ready, 3)
                prefix(equal, 0, 2)
                prefix(above, None, 4)
                pe.wait_ge(ready, 4)
                prefix(chosen, 0, 2)
                pe.wait_ge(ready, 5)
                with pe.Fori(0, E8 // EH) as c:
                    pe.wait_ge(hot_ready, c + 1)
                    for t in range(TILES):
                        last = pe.matmul(ps[:, 0, 0:2 * HI * EH], lo_hot[:, :, :, t].rearrange("p e l -> p (e l)"),
                                         hi_val[:, :, :, :, t].rearrange("p v h e -> p (v h e)"), start=(t == 0), stop=(t == TILES - 1))
                    last.then_inc(idx_ps, 1)

            @block.vector
            def _(dve):
                def put(ins, n):
                    ins.then_inc(dve_n, 1)
                    dve.wait_ge(dve_n, AT[n])
                dve.wait_ge(setup, 2)
                dve.tensor_reduce(fold[:, :], ident[:, :].rearrange("p (i e) -> p e i", e=E8), AX.X, ALU.add)
                put(dve.tensor_tensor(logits[:, :, :].rearrange("p (b t) e -> p b t e", t=2), logits[:, :, :].rearrange("p (b t) e -> p b t e", t=2),
                                      dup[:, :].rearrange("p (a t c) -> p a t c", a=1, c=1).to_broadcast([R, IMAGES, 2, E8]), ALU.add), "masked")
                dve.tensor_copy(same[:, :].rearrange("p (i e) -> p i e", e=E8), fold[:, :].rearrange("p (a e) -> p a e", a=1).to_broadcast([128, 128 // E8, E8]))
                dve.wait_ge(pe_n, 1)
                put(dve.tensor_reduce(colmax[:, :], ps[:, 0:2, 0:TB * R // 2], AX.XY, ALU.max), "colmax")
                dve.wait_ge(pe_n, 2)
                put(dve.tensor_reduce(negmax8[:, :], ps[0:1, 2, 0:128].rearrange("p (i e) -> p e i", e=E8), AX.X, ALU.max, negate=True), "negmax")
                put(dve.tensor_copy(row[:, :].rearrange("p (i e) -> p i e", e=E8), negmax8[:, :].rearrange("p (a e) -> p a e", a=1).to_broadcast([1, 128 // E8, E8])), "row")
                dve.wait_ge(pe_n, 3)
                put(dve.tensor_copy(nmax[:, :], ps[:, 3, 0:1]), "nmax")
                dve.wait_ge(pe_n, 4)
                put(dve.reciprocal(rsum[:, :], ps[:, 2, 0:1]), "rsum")
                put(dve.tensor_scalar(pT[:, :], expd[:, :], rsum[:, 0:1], None, ALU.mult), "pT")
                dve.wait_ge(pe_n, 5)
                dve.wait_ge(setup, SETUP)
                put(dve.tensor_copy(pm[:, :, :].rearrange("p t e -> p (t e)"), ps_flat[0:R, 2048:2048 + TILES * E8]), "pm_raw")
                put(dve.tensor_tensor(pm[:, :, :].rearrange("p (b t) e -> p b t e", t=2), pm[:, :, :].rearrange("p (b t) e -> p b t e", t=2),
                                      dup1[:, :].rearrange("p (a t c) -> p a t c", a=1, c=1).to_broadcast([R, IMAGES, 2, E8]), ALU.add), "pm")

                put(dve.memset(low[:, :], 2.0 ** -126), "low0")

                def try_cand(n):
                    dve.wait_ge(cand_ready, n)
                    dve.tensor_scalar(over[:, :], pT[:, :], cand[:, 0:1], None, ALU.is_ge, ALU.add, accum_out=count[:, 0:1]).then_inc(counted, 1)
                for i in range(7):
                    dve.tensor_scalar(cand[:, :], low[:, :], float(2.0 ** (64 >> i)), None, ALU.mult).then_inc(cand_ready, 1)
                    try_cand(i + 1)
                    dve.wait_ge(total, i + 1)
                    dve.tensor_scalar(flag[:, :], ps[:, 6, 0:1], CAP - 0.5, float(2.0 ** (64 >> i)) - 1.0, ALU.is_ge, ALU.mult).then_inc(flagged, 1)
                    dve.wait_ge(flagged, 2 * i + 1)
                    dve.scalar_tensor_tensor(low[:, :], flag[:, :], 1.0, low[:, :], ALU.add, ALU.mult).then_inc(flagged, 1)
                    dve.wait_ge(flagged, 2 * i + 2)
                dve.tensor_scalar(step[:, :], low[:, :], 0.5, None, ALU.mult).then_inc(flagged, 1)
                dve.tensor_scalar(cand[:, :], low[:, :], 1.5, None, ALU.mult).then_inc(cand_ready, 1)
                dve.wait_ge(flagged, 15)
                with dve.Fori(0, MANTISSA - 1) as i:
                    try_cand(i + 8)
                    dve.wait_ge(total, i + 8)
                    dve.tensor_scalar(flag[:, :], ps[:, 6, 0:1], CAP - 0.5, 0.5, ALU.is_ge, ALU.subtract).then_inc(flagged, 1)
                    dve.wait_ge(flagged, i * 2 + 16)
                    dve.scalar_tensor_tensor(cand[:, :], flag[:, :], step[:, 0:1], cand[:, :], ALU.mult, ALU.add).then_inc(cand_ready, 1)
                    dve.wait_ge(cand_ready, i + 9)
                    dve.tensor_scalar(step[:, :], step[:, :], 0.5, None, ALU.mult).then_inc(flagged, 1)
                    dve.wait_ge(flagged, i * 2 + 17)
                try_cand(7 + MANTISSA)
                F0 = 15 + 2 * (MANTISSA - 1)
                dve.wait_ge(total, 7 + MANTISSA)
                dve.tensor_scalar(flag[:, :], ps[:, 6, 0:1], CAP - 0.5, 1.0, ALU.is_ge, ALU.subtract).then_inc(flagged, 1)
                dve.wait_ge(flagged, F0 + 1)
                dve.scalar_tensor_tensor(cand[:, :], flag[:, :], step[:, 0:1], cand[:, :], ALU.mult, ALU.add).then_inc(cand_ready, 1)
                try_cand(8 + MANTISSA)
                dve.wait_ge(total, 8 + MANTISSA)
                dve.tensor_scalar(flag[:, :], ps[:, 6, 0:1], CAP - 0.5, None, ALU.is_ge).then_inc(flagged, 1)
                dve.wait_ge(flagged, F0 + 2)
                dve.tensor_tensor(low[:, :], flag[:, :], cand[:, :], ALU.mult).then_inc(ready, 1)
                dve.wait_ge(turned, 1)
                dve.tensor_copy(row8[:, :], ps[0:1, 7, 0:E8]).then_inc(ready, 1)
                dve.wait_ge(turned, 2)
                dve.tensor_copy(thr[:, :], ps[0:R, 6, 0:E8]).then_inc(flagged, 1)
                dve.wait_ge(flagged, F0 + 3)
                wide_thr = thr[:, :].rearrange("p (a e) -> p a e", a=1).to_broadcast([R, TILES, E8])
                dve.tensor_tensor(above[:, :, :], pm[:, :, :], wide_thr, ALU.is_gt)
                dve.tensor_tensor(equal[:, :, :], pm[:, :, :], wide_thr, ALU.is_equal).then_inc(ready, 1)

                def bank(i):
                    return ps_flat[0:R, i * 512:i * 512 + TILES * E8].rearrange("p (t e) -> p t e", e=E8)

                def ranks(f0):
                    for e in range(E8):
                        last = dve.tensor_tensor_scan(running[:, :, e], ones[0:R, 0:TILES], bank(2)[:, :, e], 0.0, ALU.mult, ALU.add)
                    last.then_inc(flagged, 1)
                    dve.wait_ge(flagged, f0 + 1)
                    dve.tensor_tensor(rank[:, :, :], bank(2), running[:, :, :], ALU.subtract).then_inc(flagged, 1)
                    dve.wait_ge(flagged, f0 + 2)
                    dve.tensor_tensor(rank[:, :, :], bank(0), rank[:, :, :], ALU.subtract).then_inc(flagged, 1)
                    dve.wait_ge(flagged, f0 + 3)

                dve.wait_ge(turned, 4)
                dve.tensor_reduce(taken[:, :], bank(4).rearrange("p t e -> p e t"), AX.X, ALU.add).then_inc(flagged, 1)
                dve.wait_ge(flagged, F0 + 4)
                dve.tensor_scalar(room[:, :], taken[:, :], -1.0, float(CAP), ALU.mult, ALU.add).then_inc(flagged, 1)
                dve.wait_ge(flagged, F0 + 5)
                ranks(F0 + 5)
                dve.tensor_tensor(rank[:, :, :], rank[:, :, :], room[:, :].rearrange("p (a e) -> p a e", a=1).to_broadcast([R, TILES, E8]), ALU.is_lt).then_inc(flagged, 1)
                dve.wait_ge(flagged, F0 + 9)
                dve.tensor_tensor(rank[:, :, :], rank[:, :, :], equal[:, :, :], ALU.mult).then_inc(flagged, 1)
                dve.wait_ge(flagged, F0 + 10)
                dve.tensor_tensor(chosen[:, :, :], rank[:, :, :], above[:, :, :], ALU.add).then_inc(ready, 1)
                dve.wait_ge(turned, 5)
                ranks(F0 + 10)
                dve.tensor_scalar(running[:, :, :], chosen[:, :, :], -4.0 * CAP, 4.0 * CAP, ALU.mult, ALU.add).then_inc(ready, 1)
                dve.wait_ge(ready, 5)
                dve.tensor_tensor(slot_i[:, :, :], rank[:, :, :], running[:, :, :], ALU.add).then_inc(flagged, 1)
                dve.wait_ge(flagged, F0 + 14)
                dve.tensor_scalar(slot_h[:, :, :], slot_i[:, :, :], 6, None, ALU.arith_shift_right).then_inc(flagged, 1)
                dve.wait_ge(flagged, F0 + 15)
                dve.tensor_copy(hi_b[:, :, :].rearrange("p e t -> p t e"), slot_h[:, :, :])
                dve.tensor_scalar(slot_i[:, :, :], slot_i[:, :, :], LO - 1, None, ALU.bitwise_and).then_inc(flagged, 1)
                dve.wait_ge(flagged, F0 + 16)
                dve.tensor_copy(lo_b[:, :, :].rearrange("p e t -> p t e"), slot_i[:, :, :]).then_inc(flagged, 1)
                dve.wait_ge(flagged, F0 + 17)
                with dve.Fori(0, E8 // EH) as c:
                    lo_c, hi_c = (b[:, bass.ds(c * EH, EH), :] for b in (lo_b, hi_b))
                    for i in range(HI):
                        last = dve.tensor_scalar(hi_hot[:, i, :, :], hi_c, float(i), None, ALU.is_equal)
                    last.then_inc(hi_ready, 1)
                    for i in range(LO):
                        dve.tensor_scalar(lo_hot[:, :, i, :], lo_c, float(i), None, ALU.is_equal)
                    dve.wait_ge(hi_ready, c + 1)
                    for v, val in enumerate((nval, bval)):
                        last = dve.tensor_tensor(hi_val[:, v, :, :, :].rearrange("p c e t -> p (c e) t"), hi_hot[:, :, :, :].rearrange("p c e t -> p (c e) t"),
                                                 val[:, :, :].rearrange("p (a b) t -> p a (b t)", a=1).to_broadcast([R, HI * EH, TILES]), ALU.mult)
                    last.then_inc(hot_ready, 1)
                    dve.wait_ge(idx_ps, c + 1)
                    for e in range(EH):
                        rows_e = slice(e * LO, (e + 1) * LO)
                        both = ps[rows_e, 0, 0:2 * HI * EH].rearrange("p (v h e) -> p v h e", v=2, e=EH)
                        last = dve.tensor_copy(tok_b[rows_e, :], both[:, 1, :, e])
                    last.then_inc(image_ready, 1)
                    dve.wait_ge(image_ready, c + 1)
                    for e in range(EH):
                        rows_e = slice(e * LO, (e + 1) * LO)
                        both = ps[rows_e, 0, 0:2 * HI * EH].rearrange("p (v q r e) -> p v q r e", v=2, r=2, e=EH)
                        tb = tok_b[rows_e, :].rearrange("p (q r) -> p q r", r=2)
                        for r in range(2):
                            last = dve.scalar_tensor_tensor(index[rows_e, r, bass.ds(c, 1), :].rearrange("p a s -> p (a s)"), tb[:, :, r], float(NTOK),
                                                            both[:, 0, :, r, e], ALU.mult, ALU.add)
                    last.then_inc(idx_read, 1)
                    dve.wait_ge(idx_read, c + 1)
                for e in range(EH):
                    rows_e = slice(e * LO, (e + 1) * LO)
                    dve.tensor_copy(index_all[rows_e, :, :].rearrange("p (c e) s -> p c e s", e=EH)[:, :, e, :], index[rows_e, e, :, :])

        ffn(nc, A, out_rows, table_rows, index_all, ident, ones, passed)


def ffn(nc, A, out_rows, table_rows, index_all, ident, ones, passed):
    import concourse.bass as bass
    from concourse import mybir
    from contextlib import ExitStack

    f32, i32 = mybir.dt.float32, mybir.dt.int32
    ALU = mybir.AluOpType
    ACT = mybir.ActivationFunctionType
    EXPERTS, D, F = A["W1"].shape
    FC = F // 128
    SL = index_all.shape[2]
    GW = table_rows.shape[1]
    with ExitStack() as st:
        def sb(name, shape, dt=f32):
            return st.enter_context(nc.sbuf_tensor(name, shape, dt))

        def sem(name):
            return st.enter_context(nc.semaphore(name))

        w1 = sb("w1", [128, 2, F])
        w2 = sb("w2", [128, 2, FC, D])
        b1 = sb("b1", [128, 2, FC])
        b2 = sb("b2", [1, 2, D])
        from_rows = sb("from_rows", [128, 2, SL], i32)
        to_rows = sb("to_rows", [128, 2, SL], i32)
        x = sb("x_rows", [128, 2, SL, GW])
        xT = sb("xT", [128, 2, 512])
        hid = sb("hid_e", [128, 2, FC, 512])
        y = sb("y_rows", [128, 2, SL, D])
        ps = st.enter_context(nc.psum_tensor("ffn_ps", [128, 8, 512], f32))
        w_in = [sem("w_in0"), sem("w_in1")]
        gathered = [sem("gathered0"), sem("gathered1")]
        from_ready, to_ready, xT_ps, xT_ready, up_ps, hid_ready, down_ps, y_ready, added = (sem(n) for n in (
            "from_ready", "to_ready", "e_xT_ps", "e_xT_ready", "e_up_ps", "e_hid_ready", "e_down_ps", "e_y_ready", "added"))
        block = st.enter_context(nc.Block())

        W_IN = 16 * (3 + FC)

        def experts(engine, body):
            body(0)
            with engine.Fori(0, EXPERTS // 2 - 1) as q:
                body(q + 1)

        def later(q):
            return type(q) is not int

        @block.sync
        def _(sp):
            def body(q):
                for u in range(2):
                    e = q * 2 + u
                    if later(q):
                        sp.wait_ge(down_ps, q * 4 + (2 * u - 2))
                    sp.dma_start(w1[:, u, :], A["W1"][e]).then_inc(w_in[u], 16)
                    sp.dma_start(w2[:, u, :, :], A["W2"][e].rearrange("(c p) d -> p c d", p=128)).then_inc(w_in[u], 16)
                    for f in range(FC):
                        sp.dma_start(b1[:, u, f:f + 1], A["b1"][e, f * 128:(f + 1) * 128].rearrange("(p a) -> p a", a=1)).then_inc(w_in[u], 16)
                    sp.dma_start(b2[:, u, :], A["b2"][e].rearrange("(a d) -> a d", a=1)).then_inc(w_in[u], 16)
            experts(sp, body)

        @block.gpsimd
        def _(pool):
            def indices(e, dst, ready):
                pool.tensor_copy(dst, index_all[:, bass.ds(e, 1), :].rearrange("p a s -> p (a s)")).then_inc(ready, 1)
                pool.wait_ge(ready, e + 1)
                pool.sem_inc(passed, 1)

            def gather(e, u):
                if type(e) is not int or e >= 2:
                    pool.wait_ge(y_ready, e * 2 - 2)
                pool.sem_inc(passed, 1)
                indices(e, from_rows[:, u, :], from_ready)
                for i in range(SL):
                    pool.indirect_dma_start(out=x[:, u, i, :], out_offset=None, in_=table_rows,
                                            in_offset=bass.IndirectOffsetOnAxis(ap=from_rows[:, u, i:i + 1], axis=0)).then_inc(gathered[u], 16)

            def scatter(e, u):
                if type(e) is not int or e >= 1:
                    pool.wait_ge(added, e * (SL * 16))
                pool.wait_ge(y_ready, e * 2 + 2)
                pool.sem_inc(passed, 1)
                indices(e, to_rows[:, u, :], to_ready)
                for i in range(SL):
                    pool.indirect_dma_start(out=out_rows, out_offset=bass.IndirectOffsetOnAxis(ap=to_rows[:, u, i:i + 1], axis=0),
                                            in_=y[:, u, i, :], in_offset=None, compute_op=ALU.add).then_inc(added, 16)
            gather(0, 0)
            gather(1, 1)
            gather(2, 0)
            scatter(0, 0)
            gather(3, 1)
            scatter(1, 1)
            with pool.Fori(0, EXPERTS // 2 - 2) as q:
                for u in range(2):
                    gather(q * 2 + (4 + u), u)
                    scatter(q * 2 + (2 + u), u)
            scatter(EXPERTS - 2, 0)
            scatter(EXPERTS - 1, 1)
            pool.wait_ge(added, EXPERTS * SL * 16)

        @block.scalar
        def _(act):
            def turned(n, c):
                act.wait_ge(xT_ps, n + 1)
                if type(n) is not int or n >= 2:
                    act.wait_ge(up_ps, n * FC - FC)
                act.activation(xT[:, c, :], ps[:, 7 * c, :], ACT.Copy).then_inc(xT_ready, 1)

            def gelu(n, c, u, q):
                if c == 0:
                    act.wait_ge(w_in[u], q * W_IN + W_IN)
                if type(n) is not int or n >= 2:
                    act.wait_ge(down_ps, n - 1)
                for f in range(FC):
                    act.wait_ge(up_ps, n * FC + (f + 1))
                    act.activation(hid[:, c, f, :], ps[:, 1 + f, :], ACT.Gelu, bias=b1[:, u, f:f + 1]).then_inc(hid_ready, 1)

            def body(q):
                for u in range(2):
                    for c in range(2):
                        turned(q * 4 + (2 * u + c), c)
                    for c in range(2):
                        gelu(q * 4 + (2 * u + c), c, u, q)
            experts(act, body)

        @block.tensor
        def _(pe):
            def turn(q, u, c):
                n = q * 4 + (2 * u + c)
                if c == 0:
                    pe.wait_ge(gathered[u], q * (SL * 16) + SL * 16)
                if type(n) is not int or n >= 2:
                    pe.wait_ge(xT_ready, n - 1)
                for s in range(4):
                    last = pe.transpose(ps[:, 7 * c, s * 128:(s + 1) * 128], x[:, u, 4 * c + s, 0:D], ident[:, :])
                last.then_inc(xT_ps, 1)

            def up(q, u, c):
                n = q * 4 + (2 * u + c)
                if c == 0:
                    pe.wait_ge(w_in[u], q * W_IN + W_IN)
                pe.wait_ge(xT_ready, n + 1)
                for f in range(FC):
                    if type(n) is not int or n >= 1:
                        pe.wait_ge(hid_ready, n * FC + (f + 1 - FC))
                    pe.matmul(ps[:, 1 + f, :], w1[:, u, f * 128:(f + 1) * 128], xT[:, c, :], start=True, stop=True).then_inc(up_ps, 1)

            def down(q, u, c):
                n = q * 4 + (2 * u + c)
                pe.wait_ge(hid_ready, n * FC + FC)
                if type(n) is not int or n >= 2:
                    pe.wait_ge(y_ready, n - 1)
                for s in range(4):
                    dst = ps[:, 5 + c, s * D:(s + 1) * D]
                    pe.matmul(dst, ones[0:1, :], b2[0:1, u, :], start=True, stop=False)
                    for f in range(FC):
                        last = pe.matmul(dst, hid[:, c, f, s * 128:(s + 1) * 128], w2[:, u, f, :], start=False, stop=(f == FC - 1))
                last.then_inc(down_ps, 1)

            def body(q):
                for u in range(2):
                    for stage in (turn, up, down):
                        for c in range(2):
                            stage(q, u, c)
            experts(pe, body)

        @block.vector
        def _(dve):
            def body(q):
                for u in range(2):
                    if later(q):
                        dve.wait_ge(added, q * (2 * SL * 16) + (u - 1) * (SL * 16))
                    dve.wait_ge(gathered[u], q * (SL * 16) + SL * 16)
                    for c in range(2):
                        dve.wait_ge(down_ps, q * 4 + (2 * u + c + 1))
                        for s in range(4):
                            last = dve.tensor_scalar(y[:, u, 4 * c + s, :], ps[:, 5 + c, s * D:(s + 1) * D],
                                                     x[:, u, 4 * c + s, bass.ds(q * 2 + (D + u), 1)], None, ALU.mult)
                        last.then_inc(y_ready, 1)
            experts(dve, body)


def kernel(**inputs):
    import numpy as _np
    import concourse.bacc as _bacc
    from concourse import mybir as _mybir
    from concourse.bass_utils import run_bass_kernel_spmd as _run

    x = _np.asarray(inputs["x"])
    B, C, IMG, _ = x.shape
    P = 16
    G = IMG // P
    D = inputs["L0_tok_conv_w"].shape[1]
    arrays = {"x": _np.ascontiguousarray(x.reshape(B, C, G, P, G, P).transpose(1, 3, 5, 0, 2, 4)).reshape(-1, 128, B * G * G)}
    for name, a in inputs.items():
        if name != "x":
            arrays[name.replace("L0_tok_", "").replace("L0_ffn_", "")] = _np.ascontiguousarray(a)
    nc = _bacc.Bacc("TRN2", target_bir_lowering=False, num_devices=1)
    A = {n: nc.dram_tensor(f"in_{n}", a.shape, _mybir.dt.from_np(a.dtype), kind="ExternalInput").ap() for n, a in arrays.items()}
    out = nc.dram_tensor("out_dram", (B, G * G + 1, D), _mybir.dt.float32, kind="ExternalOutput").ap()
    build(nc, A, out)
    r = _run(nc, [{f"in_{n}": a for n, a in arrays.items()}], core_ids=[0])
    return r.results[0]["out_dram"]
```
